# Optimizing a Trainium2 kernel written in Bass

```python
import numpy as np
import jax
import jax.numpy as jnp

def _softmax(x, axis=-1):
    return jax.nn.softmax(x, axis=axis)

def _gelu(x):
    return jax.nn.gelu(x, approximate=True)

def _silu(x):
    return jax.nn.silu(x)

def _sigmoid(x):
    return jax.nn.sigmoid(x)

def _layernorm(x, axis=-1, eps=1e-05):
    m = jnp.mean(x, axis=axis, keepdims=True)
    v = jnp.var(x, axis=axis, keepdims=True)
    return (x - m) / jnp.sqrt(v + eps)

def _scatter_add(tgt, idx, src, axis=0):
    return tgt.at[idx].add(src)

def _segment_sum(src, seg, n):
    return jax.ops.segment_sum(src, seg, n)
kernel_name = 'mk_recurrent_d2_jaxref_r8_fc92ab'

def setup_inputs(seed: int=0):
    np.random.seed(seed)
    _w = jnp.asarray

    def _L0_attn_setup():
        import jax, jax.numpy as jnp
        import numpy as np
        B, N, D, H = (2, 256, 128, 16)
        HD = D // H
        SCALING = (D / H) ** 0.5
        EPS = 1e-05
        key = jax.random.key(seed)
        k1, k2, k3 = jax.random.split(key, 3)
        return {'z': jax.random.normal(k1, (B, N, D), dtype=jnp.float32), 'ln_scale': jnp.ones((D,), dtype=jnp.float32), 'ln_bias': jnp.zeros((D,), dtype=jnp.float32), 'w_qkv': jax.random.normal(k2, (D, 3 * D), dtype=jnp.float32) * D ** (-0.5), 'w_proj': jax.random.normal(k3, (D, D), dtype=jnp.float32) * D ** (-0.5), 'b_proj': jnp.zeros((D,), dtype=jnp.float32)}
    _L0_attn_in = _L0_attn_setup()

    def _L0_ffn_setup():
        import jax, jax.numpy as jnp
        import numpy as np
        DIM = 128

        def _reference_tuple_inner(x, W_r, W_k, W_v, mu_r, mu_k):
            B, T, C = x.shape
            x_prev = jnp.concatenate([jnp.zeros((B, 1, C), x.dtype), x[:, :-1, :]], axis=1)
            xr = mu_r * x + (1.0 - mu_r) * x_prev
            xk = mu_k * x + (1.0 - mu_k) * x_prev
            r = jax.nn.sigmoid(jnp.einsum('btc,dc->btd', xr, W_r))
            k = jnp.einsum('btc,dc->btd', xk, W_k)
            k_act = jnp.square(jax.nn.relu(k))
            out = r * jnp.einsum('btc,dc->btd', k_act, W_v)
            new_state = x[:, -1, :]
            return (out, new_state)
        key = jax.random.key(seed)
        ks = jax.random.split(key, 6)
        B, T, C = (8, 256, DIM)
        x = jax.random.normal(ks[0], (B, T, C), dtype=jnp.float32)
        s = 1.0 / np.sqrt(C)
        W_r = jax.random.uniform(ks[1], (C, C), jnp.float32, -s, s)
        W_k = jax.random.uniform(ks[2], (C, C), jnp.float32, -s, s)
        W_v = jax.random.uniform(ks[3], (C, C), jnp.float32, -s, s)
        mu_r = jax.random.uniform(ks[4], (C,), jnp.float32)
        mu_k = jax.random.uniform(ks[5], (C,), jnp.float32)
        return {'x': x, 'W_r': W_r, 'W_k': W_k, 'W_v': W_v, 'mu_r': mu_r, 'mu_k': mu_k}
    _L0_ffn_in = _L0_ffn_setup()

    def _L1_attn_setup():
        import jax, jax.numpy as jnp
        import numpy as np
        N_HEAD = 16
        N_LANDMARKS = 64
        N_ITER = 6

        def _landmarks(t, nL):
            B, nh, T, hs = t.shape
            return t.reshape(B, nh, nL, T // nL, hs).mean(axis=3)

        def _iterative_inv(K, n_iter=N_ITER):
            I = jnp.eye(K.shape[-1], dtype=K.dtype)
            denom = jnp.max(jnp.sum(K, axis=-2), axis=-1)[..., None, None]
            V = K.swapaxes(-1, -2) / denom
            for _ in range(n_iter):
                KV = K @ V
                V = 0.25 * V @ (13.0 * I - KV @ (15.0 * I - KV @ (7.0 * I - KV)))
            return V
        key = jax.random.key(seed)
        k1, k2, k3 = jax.random.split(key, 3)
        B, T, C = (4, 512, 128)
        x = jax.random.normal(k1, (B, T, C), dtype=jnp.float32)
        W_attn = jax.random.normal(k2, (C, 3 * C), dtype=jnp.float32) * (1.0 / np.sqrt(C))
        W_proj = jax.random.normal(k3, (C, C), dtype=jnp.float32) * (1.0 / np.sqrt(C))
        return {'x': x, 'W_attn': W_attn, 'W_proj': W_proj}
    _L1_attn_in = _L1_attn_setup()

    def _L1_ffn_setup():
        import jax, jax.numpy as jnp
        import numpy as np
        E = 8
        K = 2
        CAP_RATIO = 1.05
        key = jax.random.key(seed)
        ks = jax.random.split(key, 4)
        B, S, D, H = (2, 256, 128, 512)
        x = jax.random.normal(ks[0], (B, S, D), jnp.float32)
        Wg = jax.random.normal(ks[1], (E, D), jnp.float32) * 0.02
        W1 = jax.random.normal(ks[2], (E, D, H), jnp.float32) * 0.02
        b1 = jnp.zeros((E, H), jnp.float32)
        W2 = jax.random.normal(ks[3], (E, H, D), jnp.float32) * 0.02
        b2 = jnp.zeros((E, D), jnp.float32)
        return {'x': x, 'Wg': Wg, 'W1': W1, 'b1': b1, 'W2': W2, 'b2': b2}
    _L1_ffn_in = _L1_ffn_setup()
    _d = {'L0_attn_z': _L0_attn_in['z'], 'L0_attn_ln_scale': _L0_attn_in['ln_scale'], 'L0_attn_ln_bias': _L0_attn_in['ln_bias'], 'L0_attn_w_qkv': _L0_attn_in['w_qkv'], 'L0_attn_w_proj': _L0_attn_in['w_proj'], 'L0_attn_b_proj': _L0_attn_in['b_proj'], 'L0_ffn_W_r': _L0_ffn_in['W_r'], 'L0_ffn_W_k': _L0_ffn_in['W_k'], 'L0_ffn_W_v': _L0_ffn_in['W_v'], 'L0_ffn_mu_r': _L0_ffn_in['mu_r'], 'L0_ffn_mu_k': _L0_ffn_in['mu_k'], 'L1_attn_W_attn': _L1_attn_in['W_attn'], 'L1_attn_W_proj': _L1_attn_in['W_proj'], 'L1_ffn_Wg': _L1_ffn_in['Wg'], 'L1_ffn_W1': _L1_ffn_in['W1'], 'L1_ffn_b1': _L1_ffn_in['b1'], 'L1_ffn_W2': _L1_ffn_in['W2'], 'L1_ffn_b2': _L1_ffn_in['b2']}
    _x0 = _d['L0_attn_z']
    _d['L0_attn_z'] = jax.random.normal(jax.random.fold_in(jax.random.key(seed), 1), (4, 1024, 128), dtype=_x0.dtype)
    del _x0
    return _d

def reference(L0_attn_z, L0_attn_ln_scale, L0_attn_ln_bias, L0_attn_w_qkv, L0_attn_w_proj, L0_attn_b_proj, L0_ffn_W_r, L0_ffn_W_k, L0_ffn_W_v, L0_ffn_mu_r, L0_ffn_mu_k, L1_attn_W_attn, L1_attn_W_proj, L1_ffn_Wg, L1_ffn_W1, L1_ffn_b1, L1_ffn_W2, L1_ffn_b2):

    def _L0_attn_ref(z, ln_scale, ln_bias, w_qkv, w_proj, b_proj):
        import jax, jax.numpy as jnp
        import numpy as np
        B, N, D, H = (2, 256, 128, 16)
        HD = D // H
        SCALING = (D / H) ** 0.5
        EPS = 1e-05
        b, n, d = z.shape
        mu = jnp.mean(z, axis=-1, keepdims=True)
        var = jnp.mean(jnp.square(z - mu), axis=-1, keepdims=True)
        zn = (z - mu) / jnp.sqrt(var + EPS) * ln_scale + ln_bias
        qkv = zn @ w_qkv
        qkv5 = qkv.reshape(b, n, H, HD, 3)
        q = jnp.transpose(qkv5[..., 0], (0, 2, 1, 3))
        k = jnp.transpose(qkv5[..., 1], (0, 2, 1, 3))
        v = jnp.transpose(qkv5[..., 2], (0, 2, 1, 3))
        scores = jnp.einsum('bhqd,bhkd->bhqk', q, k) / SCALING
        att = jax.nn.softmax(scores, axis=-1)
        out = jnp.einsum('bhal,bhlv->bhav', att, v)
        out = jnp.transpose(out, (0, 2, 1, 3)).reshape(b, n, d)
        out = out @ w_proj + b_proj
        return z + out

    def _L0_ffn_ref(x, W_r, W_k, W_v, mu_r, mu_k):
        import jax, jax.numpy as jnp
        import numpy as np
        DIM = 128

        def _reference_tuple_inner(x, W_r, W_k, W_v, mu_r, mu_k):
            B, T, C = x.shape
            x_prev = jnp.concatenate([jnp.zeros((B, 1, C), x.dtype), x[:, :-1, :]], axis=1)
            xr = mu_r * x + (1.0 - mu_r) * x_prev
            xk = mu_k * x + (1.0 - mu_k) * x_prev
            r = jax.nn.sigmoid(jnp.einsum('btc,dc->btd', xr, W_r))
            k = jnp.einsum('btc,dc->btd', xk, W_k)
            k_act = jnp.square(jax.nn.relu(k))
            out = r * jnp.einsum('btc,dc->btd', k_act, W_v)
            new_state = x[:, -1, :]
            return (out, new_state)
        return _reference_tuple_inner(x, W_r, W_k, W_v, mu_r, mu_k)[0]

    def _L1_attn_ref(x, W_attn, W_proj):
        import jax, jax.numpy as jnp
        import numpy as np
        N_HEAD = 16
        N_LANDMARKS = 64
        N_ITER = 6

        def _landmarks(t, nL):
            B, nh, T, hs = t.shape
            return t.reshape(B, nh, nL, T // nL, hs).mean(axis=3)

        def _iterative_inv(K, n_iter=N_ITER):
            I = jnp.eye(K.shape[-1], dtype=K.dtype)
            denom = jnp.max(jnp.sum(K, axis=-2), axis=-1)[..., None, None]
            V = K.swapaxes(-1, -2) / denom
            for _ in range(n_iter):
                KV = K @ V
                V = 0.25 * V @ (13.0 * I - KV @ (15.0 * I - KV @ (7.0 * I - KV)))
            return V
        B, T, C = x.shape
        nh, nL = (N_HEAD, N_LANDMARKS)
        hs = C // nh
        qkv = x @ W_attn
        q, k, v = jnp.split(qkv, 3, axis=-1)

        def heads(t):
            return t.reshape(B, T, nh, hs).transpose(0, 2, 1, 3)
        q, k, v = (heads(q), heads(k), heads(v))
        q_l = _landmarks(q, nL)
        k_l = _landmarks(k, nL)
        L = jax.nn.softmax(jnp.einsum('bhtd,bhld->bhtl', q, k_l), axis=-1)
        P = _iterative_inv(jax.nn.softmax(jnp.einsum('bhld,bhmd->bhlm', q_l, k_l), axis=-1))
        N = jax.nn.softmax(jnp.einsum('bhld,bhtd->bhlt', q_l, k), axis=-1)
        y = L @ (P @ (N @ v))
        y = y.transpose(0, 2, 1, 3).reshape(B, T, C)
        return y @ W_proj

    def _L1_ffn_ref(x, Wg, W1, b1, W2, b2):
        import jax, jax.numpy as jnp
        import numpy as np
        E = 8
        K = 2
        CAP_RATIO = 1.05
        B, S, D = x.shape
        T = B * S
        xf = x.reshape(T, D)
        gates = jax.nn.softmax(xf @ Wg.T, axis=-1)
        topw, topi = jax.lax.top_k(gates, K)
        C = int(round(K * T * CAP_RATIO / E))
        e_ord = topi.T.reshape(-1)
        tok_ord = jnp.tile(jnp.arange(T), K)
        oh = jax.nn.one_hot(e_ord, E, dtype=jnp.int32)
        cnt = jnp.take_along_axis(jnp.cumsum(oh, 0) - oh, e_ord[:, None], 1)[:, 0]
        within = cnt < C
        pos = jnp.where(within, cnt, C)
        x_disp = xf[tok_ord]
        buf = jnp.zeros((E, C + 1, D), xf.dtype).at[e_ord, pos].add(x_disp)[:, :C]
        h = jax.nn.gelu(jnp.einsum('ecd,edh->ech', buf, W1) + b1[:, None, :], approximate=False)
        y = jnp.einsum('ech,ehd->ecd', h, W2) + b2[:, None, :]
        y_ord = y[e_ord, jnp.minimum(pos, C - 1)] * within[:, None].astype(y.dtype)
        y_tk = y_ord.reshape(K, T, D).transpose(1, 0, 2)
        cw = topw * within.reshape(K, T).T.astype(topw.dtype)
        out = jnp.einsum('tk,tkd->td', cw, y_tk)
        return out.reshape(B, S, D)
    x = L0_attn_z
    xn = _layernorm(x, axis=-1)
    s = _L0_attn_ref(xn, L0_attn_ln_scale, L0_attn_ln_bias, L0_attn_w_qkv, L0_attn_w_proj, L0_attn_b_proj)
    g = _silu(_L0_ffn_ref(xn, L0_ffn_W_r, L0_ffn_W_k, L0_ffn_W_v, L0_ffn_mu_r, L0_ffn_mu_k))
    x = x + s * g
    xn = _layernorm(x, axis=-1)
    s = _L1_attn_ref(xn, L1_attn_W_attn, L1_attn_W_proj)
    g = _silu(_L1_ffn_ref(xn, L1_ffn_Wg, L1_ffn_W1, L1_ffn_b1, L1_ffn_W2, L1_ffn_b2))
    x = x + s * g
    return x

_drawn_inputs = setup_inputs


def setup_inputs(seed=0):
    import zlib

    import numpy as np

    out = dict(_drawn_inputs(seed))
    spreads = {'L0_attn_ln_scale': (1.0, 0.6),
     'L0_attn_ln_bias': (0.0, 0.8),
     'L0_attn_b_proj': (0.0, 0.8),
     'L1_ffn_b1': (0.0, 0.8),
     'L1_ffn_b2': (0.0, 0.8)}
    factors = {'L0_attn_w_qkv': 8.0,
     'L0_attn_w_proj': 8.0,
     'L0_ffn_W_r': 6.143,
     'L0_ffn_mu_r': 8.0,
     'L1_attn_W_attn': 8.0,
     'L1_attn_W_proj': 8.0,
     'L1_ffn_Wg': 8.0,
     'L1_ffn_W1': 8.0,
     'L1_ffn_W2': 8.0}
    for name, (base, spread) in spreads.items():
        noise = np.random.default_rng([zlib.crc32(name.encode()), seed]).standard_normal(out[name].shape)
        drawn = base * np.exp(spread * noise) if base else spread * noise
        out[name] = jnp.asarray(drawn.astype(out[name].dtype))
    for name, factor in factors.items():
        out[name] = (out[name] * factor).astype(out[name].dtype)
    return out
```

```python
import concourse.bass as bass
from concourse import mybir
from contextlib import ExitStack


F32 = mybir.dt.float32
BF16 = mybir.dt.bfloat16
I32 = mybir.dt.int32
ALU = mybir.AluOpType
ACT = mybir.ActivationFunctionType
AX = mybir.AxisListType

P = 128
B, T, D, H, HD = 4, 1024, 128, 16, 8
NT = B * T // P
TB = T // P
EPS = 1e-5
ATT_SCALE = float(HD) ** -0.5
NPART = 3
ROWS = NPART * NPART * HD
KROWS = 96
HQ = 4
QUADS = B * H // HQ
LM = 64
PAIRS = H // 2
NPAIR = B * PAIRS
E, TOPK = 8, 2
CAP = int(round(TOPK * B * T * 1.05 / E))
ENTRIES = TOPK * B * T
HID = 512
HC = HID // P
BANK = 512


class Link:

    def __init__(self, eng, sem, turn=None, per=0, start=0):
        self.eng, self.sem, self.turn, self.per, self.n = eng, sem, turn, per, start

    def __call__(self, ins):
        self.n += 1
        ins.then_inc(self.sem, 1)
        self.eng.wait_ge(self.sem, self.n if self.turn is None else self.turn * self.per + self.n)

    def end(self):
        assert self.n == self.per, self.n


def at(turn, per, k):
    return turn * per + k


def over_last(ap, n):
    return ap.unsqueeze(2).broadcast_to([ap.shape[0], ap.shape[1], n])


class Program:
    pass


def make(nc, ctx, ins):
    g = Program()
    g.nc = nc
    (g.x_in, g.ln_scale, g.ln_bias, g.w_qkv, g.w_proj, g.b_proj, g.W_r, g.W_k, g.W_v, g.mu_r, g.mu_k,
     g.W_attn, g.W_proj, g.Wg, g.W1, g.b1, g.W2, g.b2, g.out) = ins
    g.sb = lambda name, shape, dt=F32: ctx.enter_context(nc.sbuf_tensor(name, shape, dt))
    sems = {}

    def sem(name):
        if name not in sems:
            sems[name] = ctx.enter_context(nc.semaphore(name))
        return sems[name]

    g.sem = sem
    g.dram = lambda name, shape, dt=F32: nc.dram_tensor(name, shape, dt, kind="Internal").ap()
    g.ps = ctx.enter_context(nc.psum_tensor("psum", [P, 8 * BANK], F32))
    g.bank = lambda k, n=1: g.ps[:, k * BANK:(k + n) * BANK]

    g.X = g.sb("x_res", [P, NT, D])
    g.XN = g.sb("x_norm", [P, NT, D])
    g.G = g.sb("gate_or_attn", [P, NT, D])

    g.ident = g.sb("ident", [P, P])
    g.wqkv0 = g.sb("wqkv0", [P, 3, P])
    g.wproj0 = g.sb("wproj0", [P, P])
    g.wrT = g.sb("wrT", [P, P])
    g.wkT = g.sb("wkT", [P, P])
    g.wvT = g.sb("wvT", [P, P])
    g.wqkv1 = g.sb("wqkv1", [P, 3 * P])
    g.wproj1 = g.sb("wproj1", [P, P])
    g.wgT = g.sb("wgT", [P, E])
    g.b1T = g.sb("b1T", [P, E * HC])
    g.cols = g.sb("cols", [P, 8])
    g.bproj = g.sb("bproj", [P, P])
    g.eps_pow = g.sb("eps_pow", [P, TB])
    g.headmask = g.sb("headmask", [P, H])

    g.q_ops = g.dram("q_ops", [QUADS, HQ, ROWS + NPART, T], BF16)
    g.k_ops = g.dram("k_ops", [QUADS, HQ, ROWS, T], BF16)
    g.v_ops = g.dram("v_ops", [QUADS, P, HQ, TB * 2 * HD])
    g.av_out = g.dram("av_out", [QUADS, HQ, 2 * HD, T])
    g.x_disp = g.dram("x_disp", [E * CAP + ENTRIES, D])
    g.y_exp = g.dram("y_exp", [E * CAP, D])
    g.q1_keep = g.dram("q1_keep", [B, P, T])
    return g


def setup(g, ctx):
    nc, sem = g.nc, g.sem
    with ExitStack() as mem:
        raw = mem.enter_context(nc.sbuf_tensor("w_raw", [P, 3 * D], F32))
        wrkv = mem.enter_context(nc.sbuf_tensor("wrkv_raw", [P, 3, D], F32))
        wg = mem.enter_context(nc.sbuf_tensor("wg_raw", [E, D], F32))
        b1raw = mem.enter_context(nc.sbuf_tensor("b1_raw", [E * HC, P], F32))
        zeros = mem.enter_context(nc.sbuf_tensor("zeros", [P, 2048], F32))
    with nc.Block() as block:

        @block.sync
        def _(sp):
            xin = g.x_in.rearrange("b (n p) d -> p (b n) d", p=P)
            for b in range(B):
                sp.dma_start(g.X[:, b * TB:(b + 1) * TB, :], xin[:, b * TB:(b + 1) * TB, :])\
                  .then_inc(sem("x_loaded"), 16)
            for i, w in enumerate((g.W_r, g.W_k, g.W_v)):
                sp.dma_start(wrkv[:, i, :], w[:, :]).then_inc(sem("w_loaded"), 16)
            sp.dma_start(wg[:, :], g.Wg[:, :]).then_inc(sem("w_loaded"), 16)
            sp.dma_start(b1raw[:, :], g.b1.rearrange("e (c p) -> (e c) p", p=P)).then_inc(sem("w_loaded"), 16)
            sp.dma_start(raw[:, :], g.w_qkv[:, :]).then_inc(sem("wqkv_loaded"), 16)
            sp.dma_start(g.wproj0[:, :], g.w_proj[:, :]).then_inc(sem("rest_loaded"), 16)
            sp.dma_start(g.wqkv1[:, :], g.W_attn[:, :]).then_inc(sem("rest_loaded"), 16)
            sp.dma_start(g.wproj1[:, :], g.W_proj[:, :]).then_inc(sem("rest_loaded"), 16)
            sp.dma_start(g.bproj[:, :], g.b_proj.rearrange("(a n) -> a n", a=1).broadcast_to([P, D]))\
              .then_inc(sem("rest_loaded"), 16)
            for i, v in enumerate((g.ln_scale, g.ln_bias, g.mu_r, g.mu_k)):
                sp.dma_start(g.cols[:, i:i + 1], v.rearrange("(p a) -> p a", a=1))\
                  .then_inc(sem("cols_loaded"), 16)
            sp.wait_ge(sem("zeros_set"), 1)
            rows = E * CAP
            flat = g.x_disp[0:rows, :].rearrange("(q r) d -> q (r d)", q=E * 5)
            for i in range(0, CAP * D // 5, 2048):
                n = min(2048, CAP * D // 5 - i)
                sp.dma_start(flat[:, i:i + n], zeros[0:E * 5, 0:n]).then_inc(sem("disp_zeroed"), 16)
            sp.dma_start(g.q_ops.rearrange("q h r t -> (q h) r t")[:, ROWS:ROWS + NPART, :],
                         zeros[0:QUADS * HQ, 0:NPART * T // 2].bitcast(BF16).rearrange("p (r t) -> p r t", r=NPART))\
              .then_inc(sem("max_rows_zeroed"), 16)
            sp.wait_ge(sem("max_rows_zeroed"), 16)
            sp.wait_ge(sem("rest_loaded"), 64)
            sp.wait_ge(sem("x_loaded"), 64)
            sp.wait_ge(sem("disp_zeroed"), 16 * -(-(CAP * D // 5) // 2048))

        @block.gpsimd
        def _(pool):
            link = Link(pool, sem("setup_pool"))
            link(nc.gpsimd.memset(g.ident[:, :], 0.0))
            nc.gpsimd.affine_select(out=g.ident[:, :], in_=g.ident[:, :], compare_op=ALU.not_equal, fill=1.0,
                                    base=0, pattern=[[-1, P]], channel_multiplier=1).then_inc(sem("ident_set"), 1)
            link(nc.gpsimd.memset(g.headmask[:, :], float(LM) / T))
            link(nc.gpsimd.affine_select(out=g.headmask[:, :], in_=g.headmask[:, :], compare_op=ALU.is_ge,
                                         fill=0.0, base=0, pattern=[[-HD, H]], channel_multiplier=1))
            link(nc.gpsimd.affine_select(out=g.headmask[:, :], in_=g.headmask[:, :], compare_op=ALU.is_ge,
                                         fill=0.0, base=HD - 1, pattern=[[HD, H]], channel_multiplier=-1))
            nc.gpsimd.memset(zeros[:, :], 0.0).then_inc(sem("zeros_set"), 1)
            nc.gpsimd.memset(g.eps_pow[:, :], -0.5)

        @block.vector
        def _(dve):
            dve.wait_ge(sem("wqkv_loaded"), 16)
            for c in range(3):
                nc.vector.tensor_copy(g.wqkv0[:, c, :], raw[:, :].rearrange("p (n c) -> p n c", c=3)[:, :, c])
            dve.wait_ge(sem("cols_loaded"), 64)
            nc.vector.tensor_scalar(g.cols[:, 4:6], g.cols[:, 2:4], -1.0, 1.0, ALU.mult, ALU.add)
            dve.wait_ge(sem("wT_ready"), 1)
            for i, dst in enumerate((g.wrT, g.wkT, g.wvT)):
                nc.vector.tensor_copy(dst[:, :], g.ps[:, i * P:(i + 1) * P])
            nc.vector.tensor_copy(g.wgT[:, :], g.ps[:, 3 * P:3 * P + E])
            nc.vector.tensor_copy(g.b1T[:, :], g.bank(1)[:, 0:E * HC])

        @block.tensor
        def _(pe):
            pe.wait_ge(sem("ident_set"), 1)
            pe.wait_ge(sem("w_loaded"), 80)
            for i in range(3):
                nc.tensor.transpose(g.ps[:, i * P:(i + 1) * P], wrkv[:, i, :], g.ident[:, :])
            nc.tensor.transpose(g.ps[:, 3 * P:3 * P + E], wg[:, :], g.ident[0:E, 0:E])
            nc.tensor.transpose(g.bank(1)[:, 0:E * HC], b1raw[:, :], g.ident[0:E * HC, 0:E * HC])\
              .then_inc(sem("wT_ready"), 1)


def layer0_inputs(g):
    nc, sem = g.nc, g.sem
    with ExitStack() as mem:
        sb = lambda name, shape, dt=F32: mem.enter_context(nc.sbuf_tensor(name, shape, dt))
        sm = sb("a_small", [P, 8, TB])
        xc = sb("a_xc", [P, TB, D])
        sq = sb("a_sq", [P, TB, D])
        xnb = sb("a_xnb", [P, TB, D])
        znb = sb("a_znb", [P, TB, D])
        xnT = sb("a_xnT", [P, T + 1])
        znT = sb("a_znT", [P, T])
        xrT = sb("a_xrT", [P, T])
        xkT = sb("a_xkT", [P, T])
        tmp = sb("a_tmp", [P, T])
        tmp2 = sb("a_tmp2", [P, T])
        res = [sb(f"a_res{c}", [P, T]) for c in "qk"]
        part = [[sb(f"a_{c}{i}", [P, T], BF16) for i in range(NPART)] for c in "qk"]
        vs = sb("a_vs", [P, H, TB, 2 * HD])
        rg = sb("a_rg", [P, T])
        ka = sb("a_ka", [P, T])
        kaT = sb("a_kaT", [P, T])
        pr = sb("a_pr", [P, T])
        sg = sb("a_sg", [P, T])
    D0, D1, D2, D3 = (g.bank(2 * i, 2) for i in range(4))
    tiles = lambda ap: ap.rearrange("p (n c) -> p n c", c=P)
    s8, mu8, ss8, v8, rstd8, t8, v28, r28 = (sm[:, i, :] for i in range(8))
    STORES = 2 * NPART * NPART + 1

    def turn_over(eng, b):
        eng.wait_ge(sem("a_stored"), at(b, 16 * STORES, 16 * STORES))
        eng.wait_ge(sem("a_gate"), at(b, 1, 1))
        eng.wait_ge(sem("a_xn_kept"), at(b, 1, 1))

    with nc.Block() as block:

        @block.vector
        def _(dve):
            nc.vector.memset(xnT[:, 0:1], 0.0)
            nc.vector.memset(vs[:, :, :, HD:2 * HD], 1.0).then_inc(sem("a_const"), 1)
            dve.wait_ge(sem("a_const"), 1)
            with dve.Fori(0, B) as b:
                link = Link(dve, sem("a_dve"), b, 9)
                x = g.X[:, bass.ds(b * TB, TB), :]
                link(nc.vector.reduce_sum(s8, x, AX.X))
                link(nc.vector.tensor_scalar(mu8, s8, 1.0 / D, None, ALU.mult))
                link(nc.vector.tensor_tensor(xc[:, :, :], x, over_last(mu8, D), ALU.subtract))
                link(nc.vector.tensor_tensor(sq[:, :, :], xc[:, :, :], xc[:, :, :], ALU.mult))
                link(nc.vector.reduce_sum(ss8, sq[:, :, :], AX.X))
                nc.vector.tensor_scalar(v8, ss8, 1.0 / D, EPS, ALU.mult, ALU.add).then_inc(sem("a_var"), 1)
                dve.wait_ge(sem("a_rstd"), at(b, 2, 1))
                nc.vector.tensor_tensor(xnb[:, :, :], xc[:, :, :], over_last(rstd8, D), ALU.mult)\
                  .then_inc(sem("a_xn"), 1)
                link(nc.vector.tensor_tensor(t8, rstd8, rstd8, ALU.mult))
                link(nc.vector.tensor_tensor(t8, t8, ss8, ALU.mult))
                nc.vector.tensor_scalar(v28, t8, 1.0 / D, EPS, ALU.mult, ALU.add).then_inc(sem("a_var"), 1)
                dve.wait_ge(sem("a_rstd"), at(b, 2, 2))
                dve.wait_ge(sem("a_xn"), at(b, 1, 1))
                nc.vector.tensor_tensor(znb[:, :, :], xnb[:, :, :], over_last(r28, D), ALU.mult)\
                  .then_inc(sem("a_zn"), 1)
                dve.wait_ge(sem("a_xnT"), at(b, 1, 1))
                for j, (dst, name) in enumerate(((xrT, "a_xr"), (xkT, "a_xk"))):
                    link(nc.vector.tensor_scalar(tmp[:, :], xnT[:, 0:T], g.cols[:, 4 + j:5 + j], None, ALU.mult))
                    nc.vector.scalar_tensor_tensor(dst[:, :], xnT[:, 1:T + 1], g.cols[:, 2 + j:3 + j], tmp[:, :],
                                                   ALU.mult, ALU.add).then_inc(sem(name), 1)
                    dve.wait_ge(sem(name), at(b, 1, 1))
                for j, src in enumerate((D2, D3)):
                    dve.wait_ge(sem("a_part1"), at(b, 2, j + 1))
                    nc.vector.tensor_tensor(res[j][:, :], src, part[j][0][:, :], ALU.subtract)\
                      .then_inc(sem("a_res"), 1)
                for j in range(2):
                    dve.wait_ge(sem("a_part2"), at(b, 2, j + 1))
                    nc.vector.tensor_tensor(part[j][2][:, :], res[j][:, :], part[j][1][:, :], ALU.subtract)\
                      .then_inc(sem("a_part3"), 1)
                dve.wait_ge(sem("a_relu"), at(b, 1, 1))
                nc.vector.tensor_tensor(kaT[:, :], ka[:, :], ka[:, :], ALU.mult).then_inc(sem("a_kact"), 1)
                dve.wait_ge(sem("a_sigr"), at(b, 1, 1))
                dve.wait_ge(sem("a_kv"), at(b, 1, 1))
                nc.vector.tensor_tensor(pr[:, :], rg[:, :], D3, ALU.mult).then_inc(sem("a_prod"), 1)
                dve.wait_ge(sem("a_prod"), at(b, 1, 1))
                dve.wait_ge(sem("a_sigp"), at(b, 1, 1))
                nc.vector.tensor_tensor(g.G[:, bass.ds(b * TB, TB), :], tiles(pr[:, :]), tiles(sg[:, :]), ALU.mult)\
                  .then_inc(sem("a_gate"), 1)
                link.end()
                turn_over(dve, b)

        @block.gpsimd
        def _(pool):
            with pool.Fori(0, B) as b:
                pool.wait_ge(sem("a_var"), at(b, 2, 1))
                nc.gpsimd.tensor_tensor(rstd8, v8, g.eps_pow[:, :], ALU.pow).then_inc(sem("a_rstd"), 1)
                pool.wait_ge(sem("a_var"), at(b, 2, 2))
                nc.gpsimd.tensor_tensor(r28, v28, g.eps_pow[:, :], ALU.pow).then_inc(sem("a_rstd"), 1)
                turn_over(pool, b)

        @block.scalar
        def _(act):
            with act.Fori(0, B) as b:
                act.wait_ge(sem("a_xn"), at(b, 1, 1))
                act.activation(g.XN[:, bass.ds(b * TB, TB), :], xnb[:, :, :], ACT.Copy).then_inc(sem("a_xn_kept"), 1)
                act.wait_ge(sem("a_xnT_ps"), at(b, 1, 1))
                act.activation(xnT[:, 1:T + 1], D0, ACT.Copy).then_inc(sem("a_xnT"), 1)
                act.wait_ge(sem("a_znT_ps"), at(b, 1, 1))
                act.activation(znT[:, :], D1, ACT.Identity, bias=g.cols[:, 1:2], scale=g.cols[:, 0:1])\
                   .then_inc(sem("a_znT"), 1)
                for j, src in enumerate((D2, D3)):
                    act.wait_ge(sem("a_qk"), at(b, 2, j + 1))
                    act.activation(part[j][0][:, :], src, ACT.Copy).then_inc(sem("a_part1"), 1)
                for j in range(2):
                    act.wait_ge(sem("a_res"), at(b, 2, j + 1))
                    act.activation(part[j][1][:, :], res[j][:, :], ACT.Copy).then_inc(sem("a_part2"), 1)
                act.wait_ge(sem("a_v"), at(b, 1, 1))
                act.activation(vs[:, :, :, 0:HD].rearrange("p h n d -> p n h d"),
                               D0.rearrange("p (n h d) -> p n h d", h=H, d=HD), ACT.Copy).then_inc(sem("a_vs"), 1)
                act.wait_ge(sem("a_kk"), at(b, 1, 1))
                act.activation(ka[:, :], D2, ACT.Relu).then_inc(sem("a_relu"), 1)
                act.wait_ge(sem("a_r"), at(b, 1, 1))
                act.activation(rg[:, :], D1, ACT.Sigmoid).then_inc(sem("a_sigr"), 1)
                act.wait_ge(sem("a_prod"), at(b, 1, 1))
                act.activation(sg[:, :], pr[:, :], ACT.Sigmoid).then_inc(sem("a_sigp"), 1)
                turn_over(act, b)

        @block.tensor
        def _(pe):
            def rows_times(dst, lhs, rhs):
                for t in range(TB):
                    last = nc.tensor.matmul(dst[:, t * P:(t + 1) * P], lhs[:, t * P:(t + 1) * P], rhs,
                                            start=True, stop=True)
                return last

            def wide(dst, lhs, rhs):
                for j in range(T // BANK):
                    last = nc.tensor.matmul(dst[:, j * BANK:(j + 1) * BANK], lhs, rhs[:, j * BANK:(j + 1) * BANK],
                                            start=True, stop=True)
                return last

            with pe.Fori(0, B) as b:
                pe.wait_ge(sem("a_xn"), at(b, 1, 1))
                for t in range(TB):
                    last = nc.tensor.transpose(D0[:, t * P:(t + 1) * P], xnb[:, t, :], g.ident[:, :])
                last.then_inc(sem("a_xnT_ps"), 1)
                pe.wait_ge(sem("a_zn"), at(b, 1, 1))
                for t in range(TB):
                    last = nc.tensor.transpose(D1[:, t * P:(t + 1) * P], znb[:, t, :], g.ident[:, :])
                last.then_inc(sem("a_znT_ps"), 1)
                pe.wait_ge(sem("a_znT"), at(b, 1, 1))
                wide(D2, g.wqkv0[:, 0, :], znT[:, :]).then_inc(sem("a_qk"), 1)
                wide(D3, g.wqkv0[:, 1, :], znT[:, :]).then_inc(sem("a_qk"), 1)
                pe.wait_ge(sem("a_xnT"), at(b, 1, 1))
                rows_times(D0, znT, g.wqkv0[:, 2, :]).then_inc(sem("a_v"), 1)
                pe.wait_ge(sem("a_xr"), at(b, 1, 1))
                rows_times(D1, xrT, g.wrT[:, :]).then_inc(sem("a_r"), 1)
                pe.wait_ge(sem("a_xk"), at(b, 1, 1))
                pe.wait_ge(sem("a_res"), at(b, 2, 1))
                wide(D2, g.wkT[:, :], xkT[:, :]).then_inc(sem("a_kk"), 1)
                pe.wait_ge(sem("a_kact"), at(b, 1, 1))
                pe.wait_ge(sem("a_res"), at(b, 2, 2))
                rows_times(D3, kaT, g.wvT[:, :]).then_inc(sem("a_kv"), 1)
                turn_over(pe, b)

        @block.sync
        def _(sp):
            with sp.Fori(0, B) as b:
                def store(ops, j, i, rows):
                    for r in rows:
                        dst = ops[bass.ds(b * (H // HQ), H // HQ), :, r * HD:(r + 1) * HD, :]
                        sp.dma_start(dst.rearrange("q h d t -> (q h) d t"), part[j][i][:, :])\
                          .then_inc(sem("a_stored"), 16)

                for i, name in ((0, "a_part1"), (1, "a_part2"), (2, "a_part3")):
                    sp.wait_ge(sem(name), at(b, 2, 2))
                    store(g.q_ops, 0, i, [NPART * i + j for j in range(NPART)])
                    store(g.k_ops, 1, i, [NPART * j + i for j in range(NPART)])
                sp.wait_ge(sem("a_vs"), at(b, 1, 1))
                sp.dma_start(g.v_ops[bass.ds(b * (H // HQ), H // HQ), :, :, :].rearrange("q p h n -> p q h n"),
                             vs[:, :, :, :].rearrange("p (q h) n c -> p q h (n c)", q=H // HQ))\
                  .then_inc(sem("a_stored"), 16)
            sp.wait_ge(sem("a_stored"), 16 * STORES * B)


SLOTS = 3
UNITS = 32
GROUPS = UNITS // 2
MAXES = 64
ITEMS = MAXES + 1
LATE = 4
LEAD = 8
MAX_BANKS = 3
E_RING = 6


def layer0_attention(g):
    nc, sem = g.nc, g.sem
    with ExitStack() as mem:
        sb = lambda name, shape, dt=F32: mem.enter_context(nc.sbuf_tensor(name, shape, dt))
        q = [sb(f"b_q{c}", [KROWS, HQ, T], BF16) for c in range(SLOTS)]
        k = [sb(f"b_k{c}", [KROWS, HQ, T], BF16) for c in range(SLOTS)]
        v = [sb(f"b_v{c}", [P, HQ * P + 2 * HD]) for c in range(SLOTS)]
        ex = sb("b_exp_ring", [P, E_RING, 2, BANK])
        acc = sb("b_acc", [P, 2, BANK])
        mx = sb("b_mx", [P, MAXES])
        m = sb("b_m", [P, HQ * TB])
        credit = sb("b_credit", [P, 6])
        neg_rest = sb("b_neg_rest", [HQ * TB, P])
        neg = sb("b_neg", [HQ * TB, NPART, P], BF16)
    AV = g.bank(3)
    LOOPED = QUADS // SLOTS - 1
    val = lambda j, per, c, n: j * (SLOTS * per) + (c * per + n)
    last_quad = lambda j, c: isinstance(j, int) and j * SLOTS + c == QUADS - 1
    beyond = lambda j, c: isinstance(j, int) and j * SLOTS + c >= QUADS
    through = lambda u: ITEMS + (u + 1 + LEAD) * ITEMS // UNITS

    def items(j, c, lo, hi):
        for n in range(lo, hi):
            cc, i = c + n // ITEMS, n % ITEMS
            if beyond(j, cc):
                if not beyond(j, cc - 1) and i == 0:
                    yield ITEMS * cc, cc - 1, None
            elif i == LATE:
                if not (isinstance(j, int) and j * SLOTS + cc == 0):
                    yield ITEMS * cc + i, cc - 1, None
            else:
                yield ITEMS * cc + i, cc, i - (i > LATE)

    with nc.Block() as block:

        @block.vector
        def _(dve):
            for c in range(SLOTS):
                nc.vector.memset(q[c][64:KROWS, :, :], 0.0)
                nc.vector.memset(k[c][64:KROWS, :, :], 1.0)
                nc.vector.memset(v[c][:, HQ * P:], 0.0).then_inc(sem("b_rows_set"), 1)
            nc.vector.memset(credit[:, 4:5], 0.0).then_inc(sem("b_exp_done"), 2)

            def item(j, n, c, block):
                count = j * (SLOTS * ITEMS) + (n + 1)
                bank = g.bank(n % MAX_BANKS)
                dve.wait_ge(sem("b_max_scores"), count)
                if block is not None:
                    if (n % ITEMS, block) == (LATE + 1, LATE) and isinstance(j, int) and j * SLOTS + c == 0:
                        nc.vector.memset(credit[:, 5:6], 0.0).then_inc(sem("b_max_done"), 1)
                    nc.vector.reduce_max(mx[:, block:block + 1], bank, AX.X)\
                      .then_inc(sem("b_max_done"), 1)
                    if block == MAXES - 1:
                        dve.wait_ge(sem("b_max_done"), count)
                        nc.vector.reduce_max(m[:, :],
                                             mx[:, :].rearrange("p (n a) -> p n a", a=2), AX.X)\
                          .then_inc(sem("b_m"), 1)
                        dve.wait_ge(sem("b_m"), val(j, 1, c, 1))
                    return
                mT = bank[0:HQ * TB, 0:P]
                if not (isinstance(j, int) and j * SLOTS + c == 0):
                    dve.wait_ge(sem("b_m_loaded"), val(j, 16 * NPART, c, 0))
                link = Link(dve, sem("b_dve"), j, 3 * SLOTS, 3 * c)
                link(nc.vector.tensor_scalar(neg[:, 0, :], mT, -1.0, None, ALU.mult))
                link(nc.vector.scalar_tensor_tensor(neg_rest[:, :], mT, -1.0, neg[:, 0, :], ALU.mult, ALU.subtract))
                link(nc.vector.tensor_copy(neg[:, 1, :], neg_rest[:, :]))
                nc.vector.tensor_tensor(neg[:, 2, :], neg_rest[:, :], neg[:, 1, :], ALU.subtract)\
                  .then_inc(sem("b_max_done"), 1)

            for it in items(0, 0, 0, through(-1)):
                item(0, *it)
            with dve.Fori(0, LOOPED) as j:
                for c in range(SLOTS):
                    for it in items(j, c, through(-1), through(UNITS - 1)):
                        item(j, *it)
            for c in range(SLOTS + 1):
                for it in items(LOOPED, c, through(-1), through(UNITS - 1)):
                    item(LOOPED, *it)

        @block.scalar
        def _(act):
            def evacuate(j, half):
                act.wait_ge(sem("b_av"), val(j, GROUPS, 0, TB * (half + 1) + 3))
                s = half % 2
                act.wait_ge(sem(f"b_stored{s}"), val(j, 16 * HQ, 0, 16 * HQ * (half // 2 + 1)))
                act.activation(acc[:, s, :], AV, ACT.Copy).then_inc(sem("b_acc"), 1)

            def quad(j, c, carry, flush):
                for u in range(UNITS):
                    n = UNITS * c + u
                    act.wait_ge(sem("b_scores"), val(j, UNITS, 0, n + 1))
                    act.wait_ge(sem("b_av"), val(j, GROUPS, 0, n // 2 + 1))
                    b = 4 + 2 * (u % 2)
                    act.activation(ex[:, n % E_RING, :, :], g.bank(b, 2).rearrange("p (h t) -> p h t", h=2),
                                   ACT.Exp, scale=ATT_SCALE).then_inc(sem("b_exp_done"), 1)
                    if u == 2 and carry:
                        evacuate(j, 2 * c - 1)
                    if u == 18:
                        evacuate(j, 2 * c)
                if flush:
                    evacuate(j, 2 * c + 1)

            with act.Fori(0, LOOPED) as j:
                for c in range(SLOTS):
                    quad(j, c, c > 0, c == SLOTS - 1)
            for c in range(SLOTS + 1):
                quad(LOOPED, c, c > 0, c == SLOTS)

        @block.tensor
        def _(pe):
            def item(j, n, c, block):
                s = c % SLOTS
                if block == 0:
                    pe.wait_ge(sem(f"b_loaded{s}"), val(j, 16, 0, 48 * (c // SLOTS + 1)))
                if not (isinstance(j, int) and j == 0 and n < MAX_BANKS):
                    pe.wait_ge(sem("b_max_done"), j * (SLOTS * ITEMS) + (n - MAX_BANKS + 1))
                if block is None:
                    pe.wait_ge(sem("b_m"), val(j, 1, c, 1))
                    nc.tensor.transpose(g.bank(n % MAX_BANKS)[0:HQ * TB, 0:P], m[:, :], g.ident[:, :])\
                      .then_inc(sem("b_max_scores"), 1)
                    return
                h, t, half = block // 16, block // 2 % TB, block % 2
                counts = 2 if isinstance(j, int) and j * SLOTS + c == 0 and block == LATE - 1 else 1
                nc.tensor.matmul(g.bank(n % MAX_BANKS), q[s][:, h, t * P:(t + 1) * P],
                                 k[s][:, h, half * BANK:(half + 1) * BANK], start=True, stop=True)\
                  .then_inc(sem("b_max_scores"), counts)

            def times_v(j, c, group):
                s, half, kb = c % SLOTS, group // TB, group % TB
                n = UNITS * c + 2 * group
                pe.wait_ge(sem("b_exp_done"), val(j, UNITS, 0, n + 2 + 2))
                if kb == 0:
                    pe.wait_ge(sem("b_acc"), val(j, 2, c, half + 1))
                for h in range(HQ):
                    e = ex[:, (n + h // 2) % E_RING, h % 2, :]
                    last = nc.tensor.matmul(g.ps[32 * h:32 * h + 32, 3 * BANK:4 * BANK],
                                            v[s][:, h * P + kb * 2 * HD:h * P + kb * 2 * HD + 32], e,
                                            start=(kb == 0), stop=(kb == TB - 1))
                last.then_inc(sem("b_av"), 1)

            def quad(j, c, carry, flush):
                s = c % SLOTS
                for u in range(UNITS):
                    n = UNITS * c + u
                    half, kb, pair = u // 16, u // 2 % TB, u % 2
                    if u == 0:
                        pe.wait_ge(sem("b_m_loaded"), val(j, 16 * NPART, c, 16 * NPART))
                    todo = list(items(j, c, through(u - 1), through(u)))
                    pe.wait_ge(sem("b_exp_done"), val(j, UNITS, 0, n + 1))
                    for i in range(2):
                        h = 2 * pair + i
                        last = nc.tensor.matmul(g.bank(4 + 2 * (u % 2) + i), k[s][:, h, kb * P:(kb + 1) * P],
                                                q[s][:, h, half * BANK:(half + 1) * BANK], start=True, stop=True)
                    last.then_inc(sem("b_scores"), 1)
                    for it in todo[:1]:
                        item(j, *it)
                    if u == 1 and carry:
                        times_v(j, c - 1, GROUPS - 1)
                    if u >= 3 and u % 2:
                        times_v(j, c, (u - 3) // 2)
                    for it in todo[1:]:
                        item(j, *it)
                if flush:
                    times_v(j, c, GROUPS - 1)

            pe.wait_ge(sem("b_rows_set"), SLOTS)
            for it in items(0, 0, 0, through(-1)):
                item(0, *it)
            with pe.Fori(0, LOOPED) as j:
                for c in range(SLOTS):
                    quad(j, c, c > 0, c == SLOTS - 1)
            for c in range(SLOTS + 1):
                quad(LOOPED, c, c > 0, c == SLOTS)

        @block.gpsimd
        def _(pool):
            nc.gpsimd.memset(credit[:, 0:1], 0.0).then_inc(sem("b_av"), 3)
            nc.gpsimd.memset(credit[:, 1:2], 0.0).then_inc(sem("b_acc"), 1)
            for s in range(2):
                nc.gpsimd.memset(credit[:, 2 + s:3 + s], 0.0).then_inc(sem(f"b_stored{s}"), 16 * HQ)

        @block.sync
        def _(sp):
            def load(quad, c):
                one = bass.ds(quad, 1)
                sp.dma_start(q[c][0:ROWS + NPART, :, :], g.q_ops[one, :, :, :].rearrange("a h r t -> (a r) h t"))\
                  .then_inc(sem(f"b_loaded{c}"), 16)
                sp.dma_start(k[c][0:ROWS, :, :], g.k_ops[one, :, :, :].rearrange("a h r t -> (a r) h t"))\
                  .then_inc(sem(f"b_loaded{c}"), 16)
                sp.dma_start(v[c][:, 0:HQ * P], g.v_ops[one, :, :, :].rearrange("a p h n -> (a p) (h n)"))\
                  .then_inc(sem(f"b_loaded{c}"), 16)

            def store_maxima(j, c):
                n = ITEMS * (c + 1) + (1 if last_quad(j, c) else LATE + 1)
                sp.wait_ge(sem("b_max_done"), j * (SLOTS * ITEMS) + n)
                for i in range(NPART):
                    dst = q[c % SLOTS][ROWS + i:ROWS + i + 1, :, :].rearrange("r h (t x) -> r (h t) x", x=P)
                    sp.dma_start(dst, neg[:, i, :]).then_inc(sem("b_m_loaded"), 16)

            def store_half(j, c, half):
                sp.wait_ge(sem("b_acc"), val(j, 2, c, half + 1 + 1))
                for h in range(HQ):
                    dst = g.av_out[bass.ds(j * SLOTS + c, 1), h, :, half * BANK:(half + 1) * BANK]
                    sp.dma_start(dst.rearrange("a r t -> (a r) t"), acc[32 * h:32 * h + 2 * HD, half, :])\
                      .then_inc(sem(f"b_stored{half}"), 16)

            def quad(j, c):
                store_half(j, c, 0)
                if not last_quad(j, c):
                    store_maxima(j, c + 1)
                store_half(j, c, 1)
                if not beyond(j, c + SLOTS):
                    sp.wait_ge(sem("b_av"), val(j, GROUPS, c, GROUPS + 3))
                    load(j * SLOTS + (c + SLOTS), c)

            sp.wait_ge(sem("b_rows_set"), SLOTS)
            for c in range(SLOTS):
                load(c, c)
            store_maxima(0, 0)
            with sp.Fori(0, LOOPED) as j:
                for c in range(SLOTS):
                    quad(j, c)
            for c in range(SLOTS + 1):
                quad(LOOPED, c)
            for s in range(2):
                sp.wait_ge(sem(f"b_stored{s}"), 16 * HQ * (QUADS + 1))


def rows_times(nc, dst, lhs, rhs):
    n = rhs.shape[1]
    for t in range(TB):
        last = nc.tensor.matmul(dst[:, t * n:(t + 1) * n], lhs[:, t * P:(t + 1) * P], rhs, start=True, stop=True)
    return last


def wide(nc, dst, lhs, rhs):
    for j in range(T // BANK):
        last = nc.tensor.matmul(dst[:, j * BANK:(j + 1) * BANK], lhs, rhs[:, j * BANK:(j + 1) * BANK],
                                start=True, stop=True)
    return last


def heads_of(ap, mask, n):
    return ap.unsqueeze(1).broadcast_to([P, H, n]), over_last(mask, n)


def layer0_outputs(g):
    nc, sem = g.nc, g.sem
    g.LG = g.sb("logits", [P, NT, E])
    g.KS = g.sb("k_softmax", [P, NPAIR, LM])
    g.NV = g.sb("nv", [P, NPAIR, HD])
    g.KL = g.sb("kl_sums", [P, B, LM])
    with ExitStack() as mem:
        sb = lambda name, shape, dt=F32: mem.enter_context(nc.sbuf_tensor(name, shape, dt))
        num = sb("c_num", [P, T])
        den = sb("c_den", [P, T])
        oT = sb("c_oT", [P, T])
        sm = sb("c_small", [P, 8, TB])
        t1 = sb("c_t1", [P, TB, D])
        xb = sb("c_xb", [P, TB, D])
        xc = sb("c_xc", [P, TB, D])
        xnb = sb("c_xnb", [P, TB, D])
        xT = sb("c_xT", [P, T])
        qT = sb("c_qT", [P, T])
        kT = sb("c_kT", [P, T])
        v1 = sb("c_v1", [P, TB, D])
        qsum = sb("c_qsum", [P, LM])
        kl = sb("c_kl", [P, LM])
        qlm = sb("c_qlm", [P, H, LM])
        kx = sb("c_kx", [P, PAIRS, LM])
        ke = sb("c_ke", [P, PAIRS, LM])
        en = sb("c_en", [P, 2, T])
        enT = sb("c_enT", [P, 2, TB, P])
        nm = sb("c_nm", [P, PAIRS])
        nden = sb("c_nden", [P, PAIRS])
        nrec = sb("c_nrec", [P, PAIRS])
    D0, D1, D2, D3 = (g.bank(2 * i, 2) for i in range(4))
    s8, mu8, ss8, v8, rstd8, kmx, ksum, krec = (sm[:, i, :] for i in range(8))
    tiles = lambda ap: ap.rearrange("p (n c) -> p n c", c=P)
    KPS = g.ps[:, 0:PAIRS * LM].rearrange("p (n c) -> p n c", c=LM)

    def turn_over(eng, b):
        for name, per in (("c_nv_kept", 2 * PAIRS), ("c_K", 1), ("c_lg_kept", 1), ("c_xn_kept", 1), ("c_x_kept", 1)):
            eng.wait_ge(sem(name), at(b, per, per))
        eng.wait_ge(sem("c_q_kept"), at(b, 16, 16))

    with nc.Block() as block:

        @block.vector
        def _(dve):
            with dve.Fori(0, B) as b:
                link = Link(dve, sem("c_dve"), b, 14)
                mine = bass.ds(b * TB, TB)
                dve.wait_ge(sem("c_av"), at(b, 32, 32))
                link(nc.vector.reciprocal(den[:, :], den[:, :]))
                nc.vector.tensor_tensor(oT[:, :], num[:, :], den[:, :], ALU.mult).then_inc(sem("c_oT"), 1)
                dve.wait_ge(sem("c_s"), at(b, 1, 1))
                link(nc.vector.tensor_tensor(t1[:, :, :], tiles(D0), g.bproj[:, :].unsqueeze(1).broadcast_to([P, TB, D]),
                                             ALU.add))
                link(nc.vector.tensor_tensor(t1[:, :, :], t1[:, :, :], g.XN[:, mine, :], ALU.add))
                link(nc.vector.tensor_tensor(t1[:, :, :], t1[:, :, :], g.G[:, mine, :], ALU.mult))
                nc.vector.tensor_tensor(xb[:, :, :], g.X[:, mine, :], t1[:, :, :], ALU.add).then_inc(sem("c_x"), 1)
                dve.wait_ge(sem("c_x"), at(b, 1, 1))
                link(nc.vector.reduce_sum(s8, xb[:, :, :], AX.X))
                link(nc.vector.tensor_scalar(mu8, s8, 1.0 / D, None, ALU.mult))
                link(nc.vector.tensor_tensor(xc[:, :, :], xb[:, :, :], over_last(mu8, D), ALU.subtract))
                link(nc.vector.tensor_tensor(t1[:, :, :], xc[:, :, :], xc[:, :, :], ALU.mult))
                link(nc.vector.reduce_sum(ss8, t1[:, :, :], AX.X))
                nc.vector.tensor_scalar(v8, ss8, 1.0 / D, EPS, ALU.mult, ALU.add).then_inc(sem("c_var"), 1)
                dve.wait_ge(sem("c_rstd"), at(b, 1, 1))
                nc.vector.tensor_tensor(xnb[:, :, :], xc[:, :, :], over_last(rstd8, D), ALU.mult)\
                  .then_inc(sem("c_xn"), 1)
                dve.wait_ge(sem("c_qT"), at(b, 1, 1))
                link(nc.vector.reduce_sum(qsum[:, :], qT[:, :].rearrange("p (n c) -> p n c", n=LM), AX.X))
                nc.vector.tensor_tensor(qlm[:, :, :], *heads_of(qsum[:, :], g.headmask[:, :], LM), ALU.mult)\
                  .then_inc(sem("c_landmarks"), 1)
                dve.wait_ge(sem("c_kT"), at(b, 1, 1))
                ksums = g.KL[:, bass.ds(b, 1), :].rearrange("p a n -> p (a n)")
                link(nc.vector.reduce_sum(ksums, kT[:, :].rearrange("p (n c) -> p n c", n=LM), AX.X))
                nc.vector.tensor_scalar(kl[:, :], ksums, float(LM) / T, None, ALU.mult).then_inc(sem("c_landmarks"), 1)
                dve.wait_ge(sem("c_K_ps"), at(b, 1, 1))
                link(nc.vector.reduce_max(kmx, KPS, AX.X))
                nc.vector.tensor_tensor(kx[:, :, :], KPS, over_last(kmx, LM), ALU.subtract).then_inc(sem("c_kx"), 1)
                dve.wait_ge(sem("c_ke"), at(b, 1, 1))
                link(nc.vector.reduce_sum(ksum, ke[:, :, :], AX.X))
                link(nc.vector.reciprocal(krec, ksum))
                nc.vector.tensor_tensor(g.KS[:, bass.ds(b * PAIRS, PAIRS), :], ke[:, :, :], over_last(krec, LM),
                                        ALU.mult).then_inc(sem("c_K"), 1)

                def nv_out(p):
                    dve.wait_ge(sem("c_nv"), at(b, PAIRS, p + 1))
                    for i in range(2):
                        r = slice(LM * i, LM * i + LM)
                        c = (p % 2) * BANK + (2 * p + i) * HD
                        nc.vector.tensor_scalar(g.NV[r, bass.ds(b * PAIRS + p, 1), :].rearrange("p a d -> p (a d)"),
                                                g.ps[r, c:c + HD], nrec[r, p:p + 1], None, ALU.mult)\
                          .then_inc(sem("c_nv_kept"), 1)

                for p in range(PAIRS):
                    dve.wait_ge(sem("c_n_ps"), at(b, PAIRS, p + 1))
                    nc.vector.reduce_max(nm[:, p:p + 1], (D1, D2)[p % 2], AX.X, negate=True).then_inc(sem("c_nm"), 1)
                    if p >= 1:
                        dve.wait_ge(sem("c_en"), at(b, PAIRS, p))
                        nc.vector.reciprocal(nrec[:, p - 1:p], nden[:, p - 1:p]).then_inc(sem("c_nrec"), 1)
                        dve.wait_ge(sem("c_nrec"), at(b, PAIRS, p))
                    if p >= 2:
                        nv_out(p - 2)
                dve.wait_ge(sem("c_en"), at(b, PAIRS, PAIRS))
                nc.vector.reciprocal(nrec[:, PAIRS - 1:PAIRS], nden[:, PAIRS - 1:PAIRS]).then_inc(sem("c_nrec"), 1)
                dve.wait_ge(sem("c_nrec"), at(b, PAIRS, PAIRS))
                nv_out(PAIRS - 2)
                nv_out(PAIRS - 1)
                link.end()
                turn_over(dve, b)

        @block.gpsimd
        def _(pool):
            with pool.Fori(0, B) as b:
                pool.wait_ge(sem("c_var"), at(b, 1, 1))
                nc.gpsimd.tensor_tensor(rstd8, v8, g.eps_pow[:, :], ALU.pow).then_inc(sem("c_rstd"), 1)
                turn_over(pool, b)

        @block.scalar
        def _(act):
            with act.Fori(0, B) as b:
                act.wait_ge(sem("c_x"), at(b, 1, 1))
                act.activation(g.X[:, bass.ds(b * TB, TB), :], xb[:, :, :], ACT.Copy).then_inc(sem("c_x_kept"), 1)
                act.wait_ge(sem("c_xn"), at(b, 1, 1))
                act.activation(g.XN[:, bass.ds(b * TB, TB), :], xnb[:, :, :], ACT.Copy).then_inc(sem("c_xn_kept"), 1)
                act.wait_ge(sem("c_xT_ps"), at(b, 1, 1))
                act.activation(xT[:, :], D0, ACT.Copy).then_inc(sem("c_xT"), 1)
                act.wait_ge(sem("c_q_ps"), at(b, 1, 1))
                act.activation(qT[:, :], D1, ACT.Copy).then_inc(sem("c_qT"), 1)
                act.wait_ge(sem("c_k_ps"), at(b, 1, 1))
                act.activation(kT[:, :], D2, ACT.Copy).then_inc(sem("c_kT"), 1)
                act.wait_ge(sem("c_v_ps"), at(b, 1, 1))
                act.activation(v1[:, :, :], tiles(D3), ACT.Copy).then_inc(sem("c_v"), 1)
                act.wait_ge(sem("c_lg"), at(b, 1, 1))
                act.activation(g.LG[:, bass.ds(b * TB, TB), :],
                               g.ps[:, BANK:BANK + TB * E].rearrange("p (n e) -> p n e", e=E), ACT.Copy)\
                   .then_inc(sem("c_lg_kept"), 1)
                act.wait_ge(sem("c_kx"), at(b, 1, 1))
                act.activation(ke[:, :, :], kx[:, :, :], ACT.Exp).then_inc(sem("c_ke"), 1)

                def transposed_out(p):
                    act.wait_ge(sem("c_enT_ps"), at(b, PAIRS, p + 1))
                    if p >= 2:
                        act.wait_ge(sem("c_nv"), at(b, PAIRS, p - 1))
                    act.activation(enT[:, p % 2, :, :], tiles(D3), ACT.Copy).then_inc(sem("c_enT"), 1)

                for p in range(PAIRS):
                    act.wait_ge(sem("c_nm"), at(b, PAIRS, p + 1))
                    if p >= 2:
                        act.wait_ge(sem("c_enT_ps"), at(b, PAIRS, p - 1))
                    act.activation(en[:, p % 2, :], (D1, D2)[p % 2], ACT.Exp, bias=nm[:, p:p + 1],
                                   accum_out=nden[:, p:p + 1]).then_inc(sem("c_en"), 1)
                    if p >= 1:
                        transposed_out(p - 1)
                transposed_out(PAIRS - 1)
                turn_over(act, b)

        @block.tensor
        def _(pe):
            with pe.Fori(0, B) as b:
                pe.wait_ge(sem("c_oT"), at(b, 1, 1))
                rows_times(nc, D0, oT, g.wproj0[:, :]).then_inc(sem("c_s"), 1)
                pe.wait_ge(sem("c_xn"), at(b, 1, 1))
                for t in range(TB):
                    last = nc.tensor.transpose(D0[:, t * P:(t + 1) * P], xnb[:, t, :], g.ident[:, :])
                last.then_inc(sem("c_xT_ps"), 1)
                pe.wait_ge(sem("c_xT"), at(b, 1, 1))
                wide(nc, D1, g.wqkv1[:, 0:P], xT[:, :]).then_inc(sem("c_q_ps"), 1)
                wide(nc, D2, g.wqkv1[:, P:2 * P], xT[:, :]).then_inc(sem("c_k_ps"), 1)
                rows_times(nc, D3, xT, g.wqkv1[:, 2 * P:3 * P]).then_inc(sem("c_v_ps"), 1)
                rows_times(nc, g.bank(1), xT, g.wgT[:, :]).then_inc(sem("c_lg"), 1)
                pe.wait_ge(sem("c_landmarks"), at(b, 2, 2))
                for p in range(PAIRS):
                    last = nc.tensor.matmul(KPS[:, p, :], qlm[:, 2 * p:2 * p + 2, :].rearrange("p h n -> p (h n)"),
                                            kl[:, :], start=True, stop=True)
                last.then_inc(sem("c_K_ps"), 1)

                def n_scores(p):
                    if p >= 2:
                        pe.wait_ge(sem("c_en"), at(b, PAIRS, p - 1))
                    wide(nc, (D1, D2)[p % 2], qlm[:, 2 * p:2 * p + 2, :].rearrange("p h n -> p (h n)"), kT[:, :])\
                        .then_inc(sem("c_n_ps"), 1)

                def transposes(p):
                    pe.wait_ge(sem("c_en"), at(b, PAIRS, p + 1))
                    pe.wait_ge(sem("c_enT"), at(b, PAIRS, p)) if p else pe.wait_ge(sem("c_v"), at(b, 1, 1))
                    for t in range(TB):
                        last = nc.tensor.transpose(D3[:, t * P:(t + 1) * P], en[:, p % 2, t * P:(t + 1) * P],
                                                   g.ident[:, :])
                    last.then_inc(sem("c_enT_ps"), 1)

                def times_v(p):
                    pe.wait_ge(sem("c_enT"), at(b, PAIRS, p + 1))
                    if p >= 2:
                        pe.wait_ge(sem("c_nv_kept"), at(b, 2 * PAIRS, 2 * (p - 1)))
                    elif p == 0:
                        pe.wait_ge(sem("c_kx"), at(b, 1, 1))
                    else:
                        pe.wait_ge(sem("c_lg_kept"), at(b, 1, 1))
                    for t in range(TB):
                        last = nc.tensor.matmul(g.ps[:, (p % 2) * BANK:(p % 2) * BANK + P], enT[:, p % 2, t, :],
                                                v1[:, t, :], start=(t == 0), stop=(t == TB - 1))
                    last.then_inc(sem("c_nv"), 1)

                n_scores(0)
                for p in range(PAIRS):
                    if p + 1 < PAIRS:
                        n_scores(p + 1)
                    if p >= 1:
                        times_v(p - 1)
                    transposes(p)
                times_v(PAIRS - 1)
                turn_over(pe, b)

        @block.sync
        def _(sp):
            def load(b):
                for first, dst in ((0, num), (HD, den)):
                    src = g.av_out[bass.ds(b * (H // HQ), H // HQ), :, first:first + HD, :]
                    sp.dma_start(dst[:, :], src.rearrange("q h d t -> (q h) d t")).then_inc(sem("c_av"), 16)

            def keep_q(b):
                sp.wait_ge(sem("c_qT"), at(b, 1, 1))
                sp.dma_start(g.q1_keep[bass.ds(b, 1), :, :].rearrange("a p t -> (a p) t"), qT[:, :])\
                  .then_inc(sem("c_q_kept"), 16)

            load(0)
            with sp.Fori(0, B - 1) as b:
                keep_q(b)
                sp.wait_ge(sem("c_oT"), at(b, 1, 1))
                load(b + 1)
            keep_q(B - 1)
            sp.wait_ge(sem("c_q_kept"), 16 * B)


ITERS = 6
GR = 4
NG = NPAIR // GR


def inverse_and_routing(g):
    nc, sem = g.nc, g.sem
    g.WM = g.sb("w_landmark", [P, NPAIR, 32])
    g.CW = g.sb("choice_weight", [P, TOPK, NT])
    g.ROW = g.sb("row_taken", [P, TOPK * NT], I32)
    with ExitStack() as mem:
        sb = lambda name, shape, dt=F32: mem.enter_context(nc.sbuf_tensor(name, shape, dt))
        kb = sb("i_kb", [P, NPAIR, P])
        A = sb("i_a", [P, NPAIR, P])
        Q = sb("i_q", [P, NPAIR, P])
        X = sb("i_x", [P, NPAIR, P])
        twin = sb("i_ones", [P, P])
        eyes = sb("i_eyes", [P, 3, P])
        den = sb("i_den", [P, NPAIR])
        z = sb("i_z", [P, NPAIR, HD])
        gates = sb("r_gates", [P, NT, E])
        gx = sb("r_gx", [P, NT, E])
        eq = sb("r_eq", [P, NT, E])
        oh = sb("r_onehot", [P, TOPK, NT, E])
        s32 = sb("r_small", [P, 2, NT])
        idx = sb("r_idx", [P, TOPK, NT])
        tot = sb("r_tot", [P, 3, TOPK * NT, E])
        e64 = sb("r_e64", [P, 6, TOPK * NT])
        upper = sb("r_upper", [P, P])
        ones = sb("r_ones", [P, P])
        iint = sb("r_iota_int", [P, E + TOPK * NT], I32)
        iof = sb("r_iota", [P, E + TOPK * NT])
        rows_out = sb("r_rows", [P, TOPK * NT], I32)
    MM0, DV, AC = NG * 4, 3 * NG, 2 * NG
    grp = lambda ap, n: ap[:, n * GR:(n + 1) * GR, :]
    bankg = lambda n: g.bank(n % NG).rearrange("p (n c) -> p n c", c=P)
    eye = lambda i: eyes[:, i, :].unsqueeze(1).broadcast_to([P, GR, P])

    with nc.Block() as block:

        @block.gpsimd
        def _(pool):
            link = Link(pool, sem("i_pool"))
            link(nc.gpsimd.memset(kb[:, :, :], 0.0))
            nc.gpsimd.tensor_copy(kb[0:LM, :, 0:LM], g.KS[0:LM, :, :]).then_inc(sem("i_kb"), 1)
            pool.wait_ge(sem("i_kb"), 1)
            nc.gpsimd.tensor_copy(kb[LM:P, :, LM:P], g.KS[LM:P, :, :]).then_inc(sem("i_kb"), 1)
            pool.wait_ge(sem("i_kb"), 2)
            link(nc.gpsimd.memset(upper[:, :], 1.0))
            nc.gpsimd.affine_select(out=upper[:, :], in_=upper[:, :], compare_op=ALU.is_gt, fill=0.0,
                                    base=0, pattern=[[1, P]], channel_multiplier=-1).then_inc(sem("r_const"), 1)
            nc.gpsimd.memset(ones[:, :], 1.0).then_inc(sem("r_const"), 1)
            nc.gpsimd.iota(iint[:, 0:E], pattern=[[1, E]], base=-E, channel_multiplier=0).then_inc(sem("r_iota"), 1)
            nc.gpsimd.iota(iint[:, E:], pattern=[[P, TOPK * NT]], base=E * CAP, channel_multiplier=1)\
              .then_inc(sem("r_iota"), 1)
            pool.wait_ge(sem("r_rows"), 1)
            for k in range(TOPK):
                for t in range(NT):
                    n = k * NT + t
                    pool.indirect_dma_start(g.x_disp[:, :], bass.IndirectOffsetOnAxis(rows_out[:, n:n + 1], 0),
                                            g.XN[:, t, :], None).then_inc(sem("dispatched"), 16)
            pool.wait_ge(sem("dispatched"), 16 * TOPK * NT)

        @block.vector
        def _(dve):
            nc.vector.memset(twin[:, :], 0.0).then_inc(sem("i_twin"), 1)
            dve.wait_ge(sem("i_twin"), 1)
            nc.vector.memset(twin[0:LM, 0:LM], 1.0).then_inc(sem("i_twin"), 1)
            nc.vector.memset(twin[LM:P, LM:P], 1.0).then_inc(sem("i_twin"), 1)
            nc.vector.memset(g.WM[:, :, :], 0.0).then_inc(sem("i_wm"), 1)
            for i, f in enumerate((7.0, 15.0, 13.0)):
                nc.vector.tensor_scalar(eyes[:, i, :], g.ident[:, :], f, None, ALU.mult).then_inc(sem("i_eyes"), 1)
            dve.wait_ge(sem("i_eyes"), 3)

            link = Link(dve, sem("r_dve"))
            iota8 = iof[:, 0:E].unsqueeze(1).broadcast_to([P, NT, E])
            spread = lambda ap: over_last(ap, E)
            link(nc.vector.reduce_max(s32[:, 0, :], g.LG[:, :, :], AX.X))
            nc.vector.tensor_tensor(gx[:, :, :], g.LG[:, :, :], spread(s32[:, 0, :]), ALU.subtract)\
              .then_inc(sem("r_gx"), 1)
            dve.wait_ge(sem("r_iota"), 2)
            link(nc.vector.tensor_copy(iof[:, :], iint[:, :]))
            dve.wait_ge(sem("r_exp"), 1)
            link(nc.vector.reduce_sum(s32[:, 0, :], gates[:, :, :], AX.X))
            link(nc.vector.reciprocal(s32[:, 1, :], s32[:, 0, :]))
            link(nc.vector.tensor_tensor(gates[:, :, :], gates[:, :, :], spread(s32[:, 1, :]), ALU.mult))
            for k in range(TOPK):
                link(nc.vector.reduce_max(g.CW[:, k, :], gates[:, :, :], AX.X))
                link(nc.vector.tensor_tensor(eq[:, :, :], gates[:, :, :], spread(g.CW[:, k, :]), ALU.is_equal))
                link(nc.vector.tensor_tensor(eq[:, :, :], eq[:, :, :], iota8, ALU.mult))
                link(nc.vector.tensor_reduce(idx[:, k, :], eq[:, :, :], AX.X, ALU.min))
                link(nc.vector.tensor_tensor(oh[:, k, :, :], iota8, spread(idx[:, k, :]), ALU.is_equal))
                if k == 0:
                    link(nc.vector.scalar_tensor_tensor(gates[:, :, :], oh[:, k, :, :], -2.0, gates[:, :, :],
                                                        ALU.mult, ALU.add))
            nc.vector.memset(z[:, :, :], 0.0).then_inc(sem("r_oh"), 1)
            dve.wait_ge(sem("r_counts"), 2)
            link(nc.vector.tensor_copy(tot[:, 0, :, :], g.bank(6).rearrange("p (n e) -> p n e", e=E)))
            link(nc.vector.tensor_copy(tot[:, 1, :, :], tot[:, 0, :, :]))
            a, c, s = 1, 2, 1
            while s < TOPK * NT:
                link(nc.vector.tensor_tensor(tot[:, c, s:, :], tot[:, a, s:, :], tot[:, a, :TOPK * NT - s, :], ALU.add))
                link(nc.vector.tensor_copy(tot[:, c, :s, :], tot[:, a, :s, :]))
                a, c, s = c, a, 2 * s
            link(nc.vector.tensor_tensor(tot[:, a, :, :], tot[:, a, :, :], tot[:, 0, :, :], ALU.subtract))
            link(nc.vector.tensor_tensor(tot[:, c, :, :], g.bank(7).rearrange("p (n e) -> p n e", e=E), tot[:, a, :, :],
                                         ALU.add))
            link(nc.vector.tensor_tensor(tot[:, c, :, :], tot[:, c, :, :], oh[:, :, :, :].rearrange("p k n e -> p (k n) e"),
                                         ALU.mult))
            cnt, within, start, dump, w1, w2 = (e64[:, i, :] for i in range(6))
            flat = lambda ap: ap.rearrange("p k n -> p (k n)")
            link(nc.vector.reduce_sum(cnt, tot[:, c, :, :], AX.X))
            link(nc.vector.tensor_scalar(within, cnt, float(CAP), None, ALU.is_lt))
            link(nc.vector.tensor_tensor(flat(g.CW[:, :, :]), flat(g.CW[:, :, :]), within, ALU.mult))
            link(nc.vector.tensor_scalar(start, flat(idx[:, :, :]), float(E), float(CAP), ALU.add, ALU.mult))
            link(nc.vector.tensor_tensor(w1, start, cnt, ALU.add))
            link(nc.vector.tensor_tensor(w1, w1, iof[:, E:], ALU.subtract))
            link(nc.vector.tensor_tensor(w1, w1, within, ALU.mult))
            link(nc.vector.tensor_tensor(w1, w1, iof[:, E:], ALU.add))
            nc.vector.tensor_copy(rows_out[:, :], w1).then_inc(sem("r_rows"), 1)
            link(nc.vector.scalar_tensor_tensor(w2, cnt, float(CAP - 1), start, ALU.min, ALU.add))
            link(nc.vector.tensor_copy(g.ROW[:, :], w2))

            dve.wait_ge(sem("i_colsum"), 1)
            link(nc.vector.reduce_max(den[:, :], g.bank(0, 4).rearrange("p (n c) -> p n c", c=LM), AX.X))
            link(nc.vector.reciprocal(den[:, :], den[:, :]))
            nc.vector.memset(s32[:, 0, 0:1], 0.0).then_inc(sem("i_den"), 1)
            dve.wait_ge(sem("i_den"), 1)
            link(nc.vector.tensor_tensor(Q[:, :, :], g.ident[:, :].unsqueeze(1).broadcast_to([P, NPAIR, P]),
                                         over_last(den[:, :], P), ALU.mult))
            for n in range(NG):
                dve.wait_ge(sem("i_gram"), n + 1)
                nc.vector.tensor_tensor(grp(A, n), bankg(n), over_last(den[:, n * GR:(n + 1) * GR], P), ALU.mult)\
                  .then_inc(sem("i_dve"), 2)
            dve.wait_ge(sem("i_dve"), 2 * NG)
            for n in range(NG):
                nc.vector.scalar_tensor_tensor(grp(X, n), grp(A, n), -1.0, eye(0), ALU.mult, ALU.add)\
                  .then_inc(sem("i_dve"), 1)
            with dve.Fori(0, ITERS) as it:
                for stage in range(2):
                    for n in range(NG):
                        dve.wait_ge(sem("i_mm"), at(it, MM0, stage * NG + n + 1))
                        nc.vector.scalar_tensor_tensor(grp(X, n), bankg(n), -1.0, eye(1 + stage), ALU.mult, ALU.add)\
                          .then_inc(sem("i_dve"), 1)
                for n in range(NG):
                    dve.wait_ge(sem("i_act"), at(it, AC, AC + 2 * n + 2))
                    nc.vector.scalar_tensor_tensor(grp(X, n), grp(A, n), -1.0, eye(0), ALU.mult, ALU.add)\
                      .then_inc(sem("i_dve"), 1)
            dve.wait_ge(sem("i_z"), 1)
            nc.vector.tensor_copy(z[:, :, :], g.ps[:, 0:NPAIR * HD].rearrange("p (n d) -> p n d", d=HD))\
              .then_inc(sem("i_z_out"), 1)
            dve.wait_ge(sem("i_w"), 1)
            dve.wait_ge(sem("i_wm"), 1)
            w = g.ps[:, BANK:BANK + NPAIR * HD].rearrange("p (j r d) -> p j r d", r=2, d=HD)
            wm = g.WM[:, :, :].rearrange("p (j r) c -> p j r c", r=2)
            for r in range(2):
                for i in range(2):
                    half = slice(LM * i, LM * i + LM)
                    c = 16 * r + HD * i
                    nc.vector.tensor_copy(wm[half, :, r, c:c + HD], w[half, :, r, :]).then_inc(sem("i_wm"), 1)

        @block.scalar
        def _(act):
            act.wait_ge(sem("r_gx"), 1)
            act.activation(gates[:, :, :], gx[:, :, :], ACT.Exp).then_inc(sem("r_exp"), 1)
            for n in range(NG):
                act.wait_ge(sem("i_kt_ps"), n + 1)
                act.activation(grp(X, n), g.bank(4 + n % 2).rearrange("p (n c) -> p n c", c=P), ACT.Copy)\
                   .then_inc(sem("i_act"), 2)
            with act.Fori(0, ITERS) as it:
                for n in range(2 * NG):
                    act.wait_ge(sem("i_mm"), at(it, MM0, 2 * NG + n + 1))
                    act.activation(grp((A, Q)[n % 2], n // 2), bankg(n), ACT.Copy, scale=0.25)\
                       .then_inc(sem("i_act"), 1)

        @block.tensor
        def _(pe):
            def products(n, lhs, rhs, name="i_mm", pos=None):
                for i in range(GR):
                    p = n * GR + i
                    last = nc.tensor.matmul(bankg(n if pos is None else pos)[:, i, :], lhs[:, p, :], rhs[:, p, :],
                                            start=True, stop=True)
                last.then_inc(sem(name), 1)

            pe.wait_ge(sem("i_twin"), 3)
            for j in range(4):
                last = nc.tensor.matmul(g.bank(j), twin[:, :], g.KS[:, 8 * j:8 * j + 8, :].rearrange("p n c -> p (n c)"),
                                        start=True, stop=True)
            last.then_inc(sem("i_colsum"), 1)
            pe.wait_ge(sem("i_kb"), 2)
            for n in range(NG):
                if n >= 2:
                    pe.wait_ge(sem("i_act"), 2 * (n - 1))
                for i in range(GR):
                    last = nc.tensor.transpose(g.ps[:, (4 + n % 2) * BANK + i * P:(4 + n % 2) * BANK + i * P + P],
                                               kb[:, n * GR + i, :], g.ident[:, :])
                last.then_inc(sem("i_kt_ps"), 1)
            pe.wait_ge(sem("r_const"), 2)
            pe.wait_ge(sem("r_oh"), 1)
            both = oh[:, :, :, :].rearrange("p k n e -> p (k n e)")
            nc.tensor.matmul(g.bank(7), upper[:, :], both, start=True, stop=True).then_inc(sem("r_counts"), 1)
            nc.tensor.matmul(g.bank(6), ones[:, :], both, start=True, stop=True).then_inc(sem("r_counts"), 1)
            pe.wait_ge(sem("i_den"), 1)
            pe.wait_ge(sem("i_act"), 2 * NG)
            for n in range(NG):
                products(n, X, X, "i_gram")
            with pe.Fori(0, ITERS) as it:
                for n in range(NG):
                    pe.wait_ge(sem("i_act"), at(it, AC, max(2 * n + 1, NG + n + 1)))
                    pe.wait_ge(sem("i_dve"), at(it, DV, 2 * NG + n + 1))
                    products(n, A, X)
                for n in range(NG):
                    pe.wait_ge(sem("i_dve"), at(it, DV, DV + n + 1))
                    products(n, A, X)
                for n in range(2 * NG):
                    pe.wait_ge(sem("i_dve"), at(it, DV, DV + NG + (n // 2 if n >= NG else n) + 1))
                    if n >= NG:
                        pe.wait_ge(sem("i_act"), at(it, AC, AC + n - NG + 1))
                    products(n // 2, X, (A, Q)[n % 2], pos=n)
            pe.wait_ge(sem("i_act"), AC * (ITERS + 1))
            pe.wait_ge(sem("i_dve"), DV * (ITERS + 1))
            for p in range(NPAIR):
                last = nc.tensor.matmul(g.ps[:, p * HD:(p + 1) * HD], Q[:, p, :], g.NV[:, p, :], start=True, stop=True)
            last.then_inc(sem("i_z"), 1)
            pe.wait_ge(sem("i_z_out"), 1)
            for p in range(NPAIR):
                last = nc.tensor.matmul(g.ps[:, BANK + p * HD:BANK + (p + 1) * HD], kb[:, p, :], z[:, p, :],
                                        start=True, stop=True)
            last.then_inc(sem("i_w"), 1)


def layer1_attention(g):
    nc, sem = g.nc, g.sem
    with ExitStack() as mem:
        sb = lambda name, shape, dt=F32: mem.enter_context(nc.sbuf_tensor(name, shape, dt))
        qT = sb("f_qT", [P, T])
        klm = sb("f_klm", [P, H, LM])
        wm = sb("f_wm", [P, PAIRS, 32])
        mh = sb("f_max", [P, 2, H])
        lx = sb("f_lx", [P, 2, H, LM])
        le = sb("f_le", [P, 2, H, LM])
        ln = sb("f_ln", [P, 2, H, LM])
        lT = sb("f_lT", [P, 2, PAIRS, P])
        yT = sb("f_yT", [P, 2, P])
        sh = sb("f_sum", [P, 2, H])
        rh = sb("f_rec", [P, 2, H])

    def turn_over(eng, b):
        eng.wait_ge(sem("f_out"), at(b, TB, TB))

    with nc.Block() as block:

        @block.sync
        def _(sp):
            def load(b):
                sp.dma_start(qT[:, :], g.q1_keep[bass.ds(b, 1), :, :].rearrange("a p t -> (a p) t"))\
                  .then_inc(sem("f_q"), 16)

            load(0)
            with sp.Fori(0, B - 1) as b:
                sp.wait_ge(sem("f_scores"), at(b, TB, TB))
                load(b + 1)

        @block.vector
        def _(dve):
            with dve.Fori(0, B) as b:
                kls = g.KL[:, bass.ds(b, 1), :].rearrange("p a n -> p (a n)")
                nc.vector.tensor_tensor(klm[:, :, :], *heads_of(kls, g.headmask[:, :], LM), ALU.mult)\
                  .then_inc(sem("f_ready"), 1)
                nc.vector.tensor_copy(wm[:, :, :], g.WM[:, bass.ds(b * PAIRS, PAIRS), :]).then_inc(sem("f_ready"), 1)

                def total(t):
                    s = t % 2
                    dve.wait_ge(sem("f_le"), at(b, TB, t + 1))
                    nc.vector.reduce_sum(sh[:, s, :], le[:, s, :, :], AX.X).then_inc(sem("f_sum"), 1)
                    dve.wait_ge(sem("f_sum"), at(b, TB, t + 1))
                    nc.vector.reciprocal(rh[:, s, :], sh[:, s, :]).then_inc(sem("f_rec"), 1)

                for t in range(TB):
                    s = t % 2
                    ps = g.bank(2 * s, 2).rearrange("p (h n) -> p h n", n=LM)
                    dve.wait_ge(sem("f_scores"), at(b, TB, t + 1))
                    nc.vector.reduce_max(mh[:, s, :], ps, AX.X).then_inc(sem("f_max"), 1)
                    dve.wait_ge(sem("f_max"), at(b, TB, t + 1))
                    if t >= 2:
                        dve.wait_ge(sem("f_le"), at(b, TB, t - 1))
                    nc.vector.tensor_tensor(lx[:, s, :, :], ps, over_last(mh[:, s, :], LM), ALU.subtract)\
                      .then_inc(sem("f_lx"), 1)
                    if t >= 1:
                        total(t - 1)
                total(TB - 1)
                turn_over(dve, b)

        @block.gpsimd
        def _(pool):
            with pool.Fori(0, B) as b:
                for t in range(TB):
                    s = t % 2
                    pool.wait_ge(sem("f_rec"), at(b, TB, t + 1))
                    if t >= 2:
                        pool.wait_ge(sem("f_lT_ps"), at(b, TB, t - 1))
                    nc.gpsimd.tensor_tensor(ln[:, s, :, :], le[:, s, :, :], over_last(rh[:, s, :], LM), ALU.mult)\
                      .then_inc(sem("f_ln"), 1)
                turn_over(pool, b)

        @block.scalar
        def _(act):
            with act.Fori(0, B) as b:
                def transposed_out(t):
                    act.wait_ge(sem("f_lT_ps"), at(b, TB, t + 1))
                    if t >= 2:
                        act.wait_ge(sem("f_y"), at(b, TB, t - 1))
                    act.activation(lT[:, t % 2, :, :], g.bank(4, 2).rearrange("p (n c) -> p n c", c=P), ACT.Copy)\
                       .then_inc(sem("f_lT"), 1)

                def y_out(t):
                    act.wait_ge(sem("f_y"), at(b, TB, t + 1))
                    act.activation(yT[:, t % 2, :], g.ps[:, 6 * BANK:6 * BANK + P], ACT.Copy).then_inc(sem("f_yT"), 1)

                def s_out(t):
                    act.wait_ge(sem("f_s"), at(b, TB, t + 1))
                    act.activation(g.G[:, bass.ds(b * TB + t, 1), :].rearrange("p a d -> p (a d)"),
                                   g.ps[:, 7 * BANK:7 * BANK + P], ACT.Copy).then_inc(sem("f_out"), 1)

                for t in range(TB + 4):
                    if t < TB:
                        s = t % 2
                        act.wait_ge(sem("f_lx"), at(b, TB, t + 1))
                        if t >= 2:
                            act.wait_ge(sem("f_ln"), at(b, TB, t - 1))
                        act.activation(le[:, s, :, :], lx[:, s, :, :], ACT.Exp).then_inc(sem("f_le"), 1)
                    if 2 <= t < TB + 2:
                        transposed_out(t - 2)
                    if 3 <= t < TB + 3:
                        y_out(t - 3)
                    if 4 <= t:
                        s_out(t - 4)
                turn_over(act, b)

        @block.tensor
        def _(pe):
            with pe.Fori(0, B) as b:
                pe.wait_ge(sem("f_q"), at(b, 16, 16))
                pe.wait_ge(sem("f_ready"), at(b, 2, 2))

                def scores(t):
                    if t >= 2:
                        pe.wait_ge(sem("f_lx"), at(b, TB, t - 1))
                    for j in range(2):
                        last = nc.tensor.matmul(g.bank(2 * (t % 2) + j), qT[:, t * P:(t + 1) * P],
                                                klm[:, 8 * j:8 * j + 8, :].rearrange("p h n -> p (h n)"),
                                                start=True, stop=True)
                    last.then_inc(sem("f_scores"), 1)

                def transposes(t):
                    pe.wait_ge(sem("f_ln"), at(b, TB, t + 1))
                    if t >= 1:
                        pe.wait_ge(sem("f_lT"), at(b, TB, t))
                    for p in range(PAIRS):
                        last = nc.tensor.transpose(g.ps[:, 4 * BANK + p * P:4 * BANK + (p + 1) * P],
                                                   ln[:, t % 2, 2 * p:2 * p + 2, :].rearrange("p h n -> p (h n)"),
                                                   g.ident[:, :])
                    last.then_inc(sem("f_lT_ps"), 1)

                def y(t):
                    pe.wait_ge(sem("f_lT"), at(b, TB, t + 1))
                    if t >= 1:
                        pe.wait_ge(sem("f_yT"), at(b, TB, t))
                    for r in range(2):
                        for j in range(4):
                            last = nc.tensor.matmul(g.ps[32 * j:32 * j + 32, 6 * BANK:6 * BANK + P], wm[:, 2 * j + r, :],
                                                    lT[:, t % 2, 2 * j + r, :], start=(r == 0), stop=(r == 1))
                    last.then_inc(sem("f_y"), 1)

                def project(t):
                    pe.wait_ge(sem("f_yT"), at(b, TB, t + 1))
                    if t >= 1:
                        pe.wait_ge(sem("f_out"), at(b, TB, t))
                    nc.tensor.matmul(g.ps[:, 7 * BANK:7 * BANK + P], yT[:, t % 2, :], g.wproj1[:, :],
                                     start=True, stop=True).then_inc(sem("f_s"), 1)

                for t in range(TB + 4):
                    if t < TB:
                        scores(t)
                    if 2 <= t < TB + 2:
                        transposes(t - 2)
                    if 3 <= t < TB + 3:
                        y(t - 3)
                    if 4 <= t:
                        project(t - 4)
                turn_over(pe, b)


XT = -(-CAP // P)
LASTROWS = CAP - (XT - 1) * P
CHUNKS = [(i * CAP // 3, (i + 1) * CAP // 3) for i in range(3)]


def experts(g):
    nc, sem = g.nc, g.sem
    with ExitStack() as mem:
        sb = lambda name, shape, dt=F32: mem.enter_context(nc.sbuf_tensor(name, shape, dt))
        xe = [sb(f"e_x{c}", [P, XT, D]) for c in range(2)]
        w1 = [sb(f"e_w1{c}", [P, HID]) for c in range(2)]
        w2 = [sb(f"e_w2{c}", [P, HC, D]) for c in range(2)]
        b1 = [sb(f"e_b1{c}", [P, HC]) for c in range(2)]
        b2 = [sb(f"e_b2{c}", [P, D]) for c in range(2)]
        xT = sb("e_xT", [P, CAP])
        hT = [sb(f"e_hT{c}", [P, HC, CAP]) for c in range(2)]
        y = [sb(f"e_y{c}", [P, XT, D]) for c in range(2)]
        credit = sb("e_credit", [P, 2])
    NCH = len(CHUNKS)
    LOADS = 16 * 5
    ex = lambda j, per, c, n: j * (2 * per) + (c * per + n)
    rows = lambda t: P if t < XT - 1 else LASTROWS

    with nc.Block() as block:

        @block.sync
        def _(sp):
            def load(j, c):
                one = bass.ds(j * 2 + c, 1)
                flat = lambda ap: ap.rearrange("a p n -> (a p) n")
                first = (j * 2 + c) * CAP
                s = f"e_loaded{c}"
                sp.dma_start(xe[c][:, 0:XT - 1, :],
                             g.x_disp[bass.ds(first, (XT - 1) * P), :].rearrange("(t p) d -> p t d", p=P))\
                  .then_inc(sem(s), 16)
                sp.dma_start(xe[c][0:LASTROWS, XT - 1, :], g.x_disp[bass.ds(first + (XT - 1) * P, LASTROWS), :])\
                  .then_inc(sem(s), 16)
                sp.dma_start(w1[c][:, :], flat(g.W1[one, :, :])).then_inc(sem(s), 16)
                sp.dma_start(w2[c][:, :, :], g.W2[one, :, :].rearrange("a (c p) d -> (a p) c d", p=P))\
                  .then_inc(sem(s), 16)
                sp.dma_start(b2[c][:, :], g.b2[one, :].broadcast_to([P, D])).then_inc(sem(s), 16)

            def store(j, c):
                sp.wait_ge(sem("e_y"), ex(j, 3, c, 3))
                first = (j * 2 + c) * CAP
                sp.dma_start(g.y_exp[bass.ds(first, (XT - 1) * P), :].rearrange("(t p) d -> p t d", p=P),
                             y[c][:, 0:XT - 1, :]).then_inc(sem(f"e_stored{c}"), 16)
                sp.dma_start(g.y_exp[bass.ds(first + (XT - 1) * P, LASTROWS), :], y[c][0:LASTROWS, XT - 1, :])\
                  .then_inc(sem(f"e_stored{c}"), 16)

            for c in range(2):
                load(0, c)
            with sp.Fori(0, E // 2 - 1) as j:
                for c in range(2):
                    store(j, c)
                    load(j + 1, c)
            for c in range(2):
                store(E // 2 - 1, c)
                sp.wait_ge(sem(f"e_stored{c}"), 32 * (E // 2 + 1))

        @block.gpsimd
        def _(pool):
            for c in range(2):
                nc.gpsimd.memset(credit[:, c:c + 1], 0.0).then_inc(sem(f"e_stored{c}"), 32)

        @block.vector
        def _(dve):
            with dve.Fori(0, E // 2) as j:
                for c in range(2):
                    nc.vector.tensor_copy(b1[c][:, :], g.b1T[:, bass.ds((j * 2 + c) * HC, HC)]).then_inc(sem("e_b1"), 1)
                    for i in range(3):
                        n = 4 if i < 2 else 1
                        r = P if i < 2 else LASTROWS
                        w = n * P if i < 2 else LASTROWS
                        dve.wait_ge(sem("e_xT_ps"), ex(j, 3, c, i + 1))
                        nc.vector.tensor_copy(xT[:, i * BANK:i * BANK + w], g.ps[:, i * BANK:i * BANK + w])\
                          .then_inc(sem("e_xT"), 1)
                    dve.wait_ge(sem(f"e_stored{c}"), j * 32 + 32)
                    for i in range(3):
                        n = 4 if i < 2 else 1
                        r = P if i < 2 else LASTROWS
                        dve.wait_ge(sem("e_y_ps"), ex(j, 3, c, i + 1))
                        nc.vector.tensor_tensor(y[c][0:r, 4 * i:4 * i + n, :],
                                                g.ps[0:r, (6 + i % 2) * BANK:(6 + i % 2) * BANK + n * P]
                                                .rearrange("p (n c) -> p n c", c=P),
                                                b2[c][0:r, :].unsqueeze(1).broadcast_to([r, n, D]), ALU.add)\
                          .then_inc(sem("e_y"), 1)

        @block.scalar
        def _(act):
            with act.Fori(0, E // 2) as j:
                for c in range(2):
                    act.wait_ge(sem("e_b1"), ex(j, 1, c, 1))
                    for i in range(HC):
                        for m, (lo, hi) in enumerate(CHUNKS):
                            n = i * NCH + m
                            act.wait_ge(sem("e_h_ps"), ex(j, HC * NCH, c, n + 1))
                            act.activation(hT[c][:, i, lo:hi], g.ps[:, (3 + n % 3) * BANK:(3 + n % 3) * BANK + hi - lo],
                                           ACT.Gelu, bias=b1[c][:, i:i + 1]).then_inc(sem("e_h"), 1)

        @block.tensor
        def _(pe):
            with pe.Fori(0, E // 2) as j:
                for c in range(2):
                    pe.wait_ge(sem(f"e_loaded{c}"), j * LOADS + LOADS)
                    for t in range(XT):
                        last = nc.tensor.transpose(g.ps[:, t * P:t * P + rows(t)], xe[c][0:rows(t), t, :],
                                                   g.ident[0:rows(t), 0:rows(t)])
                        if t % 4 == 3 or t == XT - 1:
                            last.then_inc(sem("e_xT_ps"), 1)
                    pe.wait_ge(sem("e_xT"), ex(j, 3, c, 3))
                    for i in range(HC):
                        for m, (lo, hi) in enumerate(CHUNKS):
                            n = i * NCH + m
                            if n >= 3:
                                pe.wait_ge(sem("e_h"), ex(j, HC * NCH, c, n - 2))
                            nc.tensor.matmul(g.ps[:, (3 + n % 3) * BANK:(3 + n % 3) * BANK + hi - lo],
                                             w1[c][:, i * P:(i + 1) * P], xT[:, lo:hi], start=True, stop=True)\
                              .then_inc(sem("e_h_ps"), 1)
                    pe.wait_ge(sem("e_h"), ex(j, HC * NCH, c, HC * NCH))
                    for t in range(XT):
                        r = rows(t)
                        if t == 2 * 4:
                            pe.wait_ge(sem("e_y"), ex(j, 3, c, 1))
                        col = (6 + t // 4 % 2) * BANK + t % 4 * P
                        for i in range(HC):
                            last = nc.tensor.matmul(g.ps[0:r, col:col + D], hT[c][:, i, t * P:t * P + r], w2[c][:, i, :],
                                                    start=(i == 0), stop=(i == HC - 1))
                        if t % 4 == 3 or t == XT - 1:
                            last.then_inc(sem("e_y_ps"), 1)
                    pe.wait_ge(sem("e_y"), ex(j, 3, c, 3))


def combine(g):
    nc, sem = g.nc, g.sem
    with ExitStack() as mem:
        sb = lambda name, shape, dt=F32: mem.enter_context(nc.sbuf_tensor(name, shape, dt))
        yk = sb("g_y", [P, TOPK, NT, D])
        f = sb("g_f", [P, NT, D])
        sg = sb("g_sg", [P, NT, D])
    with nc.Block() as block:

        @block.gpsimd
        def _(pool):
            for t in range(NT):
                for k in range(TOPK):
                    n = k * NT + t
                    pool.indirect_dma_start(yk[:, k, t, :], None, g.y_exp[:, :],
                                            bass.IndirectOffsetOnAxis(g.ROW[:, n:n + 1], 0))\
                        .then_inc(sem(f"g_gathered{t // TB}"), 16)

        @block.vector
        def _(dve):
            link = Link(dve, sem("g_dve"))

            def finish(b):
                s = slice(b * TB, (b + 1) * TB)
                dve.wait_ge(sem("g_sg"), b + 1)
                link(nc.vector.tensor_tensor(f[:, s, :], f[:, s, :], sg[:, s, :], ALU.mult))
                link(nc.vector.tensor_tensor(f[:, s, :], f[:, s, :], g.G[:, s, :], ALU.mult))
                nc.vector.tensor_tensor(g.X[:, s, :], g.X[:, s, :], f[:, s, :], ALU.add).then_inc(sem("g_x"), 1)

            for b in range(B):
                s = slice(b * TB, (b + 1) * TB)
                dve.wait_ge(sem(f"g_gathered{b}"), 16 * TOPK * TB)
                for k in range(TOPK):
                    link(nc.vector.tensor_tensor(yk[:, k, s, :], yk[:, k, s, :], over_last(g.CW[:, k, s], D), ALU.mult))
                nc.vector.tensor_tensor(f[:, s, :], yk[:, 0, s, :], yk[:, 1, s, :], ALU.add).then_inc(sem("g_f"), 1)
                dve.wait_ge(sem("g_f"), b + 1)
                if b >= 1:
                    finish(b - 1)
            finish(B - 1)

        @block.scalar
        def _(act):
            for b in range(B):
                s = slice(b * TB, (b + 1) * TB)
                act.wait_ge(sem("g_f"), b + 1)
                act.activation(sg[:, s, :], f[:, s, :], ACT.Sigmoid).then_inc(sem("g_sg"), 1)

        @block.sync
        def _(sp):
            dst = g.out.rearrange("b (n p) d -> p (b n) d", p=P)
            for b in range(B):
                s = slice(b * TB, (b + 1) * TB)
                sp.wait_ge(sem("g_x"), b + 1)
                sp.dma_start(dst[:, s, :], g.X[:, s, :]).then_inc(sem("out_stored"), 16)
            sp.wait_ge(sem("out_stored"), 16 * B)


def two_layers(nc, *ins):
    with ExitStack() as ctx:
        g = make(nc, ctx, ins)
        setup(g, ctx)
        layer0_inputs(g)
        layer0_attention(g)
        layer0_outputs(g)
        inverse_and_routing(g)
        layer1_attention(g)
        experts(g)
        combine(g)


_INS = ['L0_attn_z', 'L0_attn_ln_scale', 'L0_attn_ln_bias', 'L0_attn_w_qkv', 'L0_attn_w_proj', 'L0_attn_b_proj',
        'L0_ffn_W_r', 'L0_ffn_W_k', 'L0_ffn_W_v', 'L0_ffn_mu_r', 'L0_ffn_mu_k', 'L1_attn_W_attn', 'L1_attn_W_proj',
        'L1_ffn_Wg', 'L1_ffn_W1', 'L1_ffn_b1', 'L1_ffn_W2', 'L1_ffn_b2']
_OUTS = [((B, T, D), 'float32')]


def kernel(**inputs):
    import numpy as _np
    import concourse.bacc as _bacc
    from concourse import mybir as _mybir
    from concourse.bass_utils import run_bass_kernel_spmd as _run

    nc = _bacc.Bacc("TRN2", target_bir_lowering=False, num_devices=1)
    arrays, args = {}, []
    for name in _INS:
        a = _np.ascontiguousarray(inputs[name])
        arrays[f"in_{name}_dram"] = a
        args.append(nc.dram_tensor(f"in_{name}_dram", a.shape, _mybir.dt.from_np(a.dtype), kind="ExternalInput").ap())
    for i, (shape, dtype) in enumerate(_OUTS):
        dt = _mybir.dt.from_np(_np.dtype(dtype))
        args.append(nc.dram_tensor(f"out_{i}_dram", shape, dt, kind="ExternalOutput").ap())
    two_layers(nc, *args)
    r = _run(nc, [arrays], core_ids=[0])
    got = tuple(r.results[0][f"out_{i}_dram"] for i in range(len(_OUTS)))
    return got[0]
```

```python
import concourse.bass as bass
from concourse import mybir
from contextlib import ExitStack


F32 = mybir.dt.float32
BF16 = mybir.dt.bfloat16
I32 = mybir.dt.int32
ALU = mybir.AluOpType
ACT = mybir.ActivationFunctionType
AX = mybir.AxisListType

P = 128
B, T, D, H, HD = 4, 1024, 128, 16, 8
NT = B * T // P
TB = T // P
EPS = 1e-5
ATT_SCALE = float(HD) ** -0.5
NPART = 3
ROWS = NPART * NPART * HD
KROWS = 96
HQ = 4
QUADS = B * H // HQ
LM = 64
PAIRS = H // 2
NPAIR = B * PAIRS
E, TOPK = 8, 2
CAP = int(round(TOPK * B * T * 1.05 / E))
ENTRIES = TOPK * B * T
HID = 512
HC = HID // P
BANK = 512


class Link:

    def __init__(self, eng, sem, turn=None, per=0, start=0):
        self.eng, self.sem, self.turn, self.per, self.n = eng, sem, turn, per, start

    def __call__(self, ins):
        self.n += 1
        ins.then_inc(self.sem, 1)
        self.eng.wait_ge(self.sem, self.n if self.turn is None else self.turn * self.per + self.n)

    def end(self):
        assert self.n == self.per, self.n


def at(turn, per, k):
    return turn * per + k


def over_last(ap, n):
    return ap.unsqueeze(2).broadcast_to([ap.shape[0], ap.shape[1], n])


class Program:
    pass


def make(nc, ctx, ins):
    g = Program()
    g.nc = nc
    (g.x_in, g.ln_scale, g.ln_bias, g.w_qkv, g.w_proj, g.b_proj, g.W_r, g.W_k, g.W_v, g.mu_r, g.mu_k,
     g.W_attn, g.W_proj, g.Wg, g.W1, g.b1, g.W2, g.b2, g.out) = ins
    g.sb = lambda name, shape, dt=F32: ctx.enter_context(nc.sbuf_tensor(name, shape, dt))
    sems = {}

    def sem(name):
        if name not in sems:
            sems[name] = ctx.enter_context(nc.semaphore(name))
        return sems[name]

    g.sem = sem
    g.dram = lambda name, shape, dt=F32: nc.dram_tensor(name, shape, dt, kind="Internal").ap()
    g.ps = ctx.enter_context(nc.psum_tensor("psum", [P, 8 * BANK], F32))
    g.bank = lambda k, n=1: g.ps[:, k * BANK:(k + n) * BANK]

    g.X = g.sb("x_res", [P, NT, D])
    g.XN = g.sb("x_norm", [P, NT, D])
    g.G = g.sb("gate_or_attn", [P, NT, D])

    g.ident = g.sb("ident", [P, P])
    g.wqkv0 = g.sb("wqkv0", [P, 3, P])
    g.wproj0 = g.sb("wproj0", [P, P])
    g.wrT = g.sb("wrT", [P, P])
    g.wkT = g.sb("wkT", [P, P])
    g.wvT = g.sb("wvT", [P, P])
    g.wqkv1 = g.sb("wqkv1", [P, 3 * P])
    g.wproj1 = g.sb("wproj1", [P, P])
    g.wgT = g.sb("wgT", [P, E])
    g.b1T = g.sb("b1T", [P, E * HC])
    g.cols = g.sb("cols", [P, 8])
    g.bproj = g.sb("bproj", [P, P])
    g.eps_pow = g.sb("eps_pow", [P, TB])
    g.mask4 = g.sb("mask4", [P, 4])
    g.headmask = g.sb("headmask", [P, H])

    g.q_ops = g.dram("q_ops", [QUADS, HQ, ROWS + NPART, T], BF16)
    g.k_ops = g.dram("k_ops", [QUADS, HQ, ROWS, T], BF16)
    g.v_ops = g.dram("v_ops", [QUADS, P, HQ, TB * 2 * HD])
    g.av_out = g.dram("av_out", [QUADS, HQ, 2 * HD, T])
    g.x_disp = g.dram("x_disp", [E * CAP + ENTRIES, D])
    g.y_exp = g.dram("y_exp", [E * CAP, D])
    g.recs = g.dram("recs", [B, H, T])
    g.q1_keep = g.dram("q1_keep", [B, P, T])
    return g


def setup(g, ctx):
    nc, sem = g.nc, g.sem
    with ExitStack() as mem:
        raw = mem.enter_context(nc.sbuf_tensor("w_raw", [P, 3 * D], F32))
        wrkv = mem.enter_context(nc.sbuf_tensor("wrkv_raw", [P, 3, D], F32))
        wg = mem.enter_context(nc.sbuf_tensor("wg_raw", [E, D], F32))
        b1raw = mem.enter_context(nc.sbuf_tensor("b1_raw", [E * HC, P], F32))
        zeros = mem.enter_context(nc.sbuf_tensor("zeros", [P, NPART * T // 2], F32))
    with nc.Block() as block:

        @block.sync
        def _(sp):
            xin = g.x_in.rearrange("b (n p) d -> p (b n) d", p=P)
            for b in range(B):
                sp.dma_start(g.X[:, b * TB:(b + 1) * TB, :], xin[:, b * TB:(b + 1) * TB, :])\
                  .then_inc(sem("setup_moved"), 16)
            for i, w in enumerate((g.W_r, g.W_k, g.W_v)):
                sp.dma_start(wrkv[:, i, :], w[:, :]).then_inc(sem("w_loaded"), 16)
            sp.dma_start(wg[:, :], g.Wg[:, :]).then_inc(sem("w_loaded"), 16)
            sp.dma_start(b1raw[:, :], g.b1.rearrange("e (c p) -> (e c) p", p=P)).then_inc(sem("w_loaded"), 16)
            sp.dma_start(raw[:, :], g.w_qkv[:, :]).then_inc(sem("w_loaded"), 16)
            sp.dma_start(g.wproj0[:, :], g.w_proj[:, :]).then_inc(sem("setup_moved"), 16)
            sp.dma_start(g.wqkv1[:, :], g.W_attn[:, :]).then_inc(sem("setup_moved"), 16)
            sp.dma_start(g.wproj1[:, :], g.W_proj[:, :]).then_inc(sem("setup_moved"), 16)
            sp.dma_start(g.bproj[:, :], g.b_proj.rearrange("(a n) -> a n", a=1).broadcast_to([P, D]))\
              .then_inc(sem("setup_moved"), 16)
            for i, v in enumerate((g.ln_scale, g.ln_bias, g.mu_r, g.mu_k)):
                sp.dma_start(g.cols[:, i:i + 1], v.rearrange("(p a) -> p a", a=1))\
                  .then_inc(sem("w_loaded"), 16)
            sp.wait_ge(sem("zeros_set"), 1)
            sp.dma_start(g.q_ops.rearrange("q h r t -> (q h) r t")[:, ROWS:ROWS + NPART, :],
                         zeros[0:QUADS * HQ, 0:NPART * T // 2].bitcast(BF16).rearrange("p (r t) -> p r t", r=NPART))\
              .then_inc(sem("setup_moved"), 16)
            sp.wait_ge(sem("setup_moved"), 16 * (B + 4 + 1))

        @block.gpsimd
        def _(pool):
            link = Link(pool, sem("pool_step"))
            link(nc.gpsimd.memset(g.ident[:, :], 0.0))
            nc.gpsimd.affine_select(out=g.ident[:, :], in_=g.ident[:, :], compare_op=ALU.not_equal, fill=1.0,
                                    base=0, pattern=[[-1, P]], channel_multiplier=1).then_inc(sem("ident_set"), 1)
            link(nc.gpsimd.memset(g.headmask[:, :], float(LM) / T))
            link(nc.gpsimd.affine_select(out=g.headmask[:, :], in_=g.headmask[:, :], compare_op=ALU.is_ge,
                                         fill=0.0, base=0, pattern=[[-HD, H]], channel_multiplier=1))
            link(nc.gpsimd.affine_select(out=g.headmask[:, :], in_=g.headmask[:, :], compare_op=ALU.is_ge,
                                         fill=0.0, base=HD - 1, pattern=[[HD, H]], channel_multiplier=-1))
            nc.gpsimd.memset(zeros[:, :], 0.0).then_inc(sem("zeros_set"), 1)
            pool.wait_ge(sem("zeros_set"), 1)
            nc.gpsimd.memset(g.eps_pow[:, :], -0.5)
            g.pool_steps = link.n

        @block.vector
        def _(dve):
            dve.wait_ge(sem("zeros_set"), 1)
            link = Link(dve, sem("dve_step"))
            link(nc.vector.reduce_sum(g.mask4[:, :], g.headmask[:, :].rearrange("p (j i) -> p i j", i=4), AX.X))
            nc.vector.tensor_scalar(g.mask4[:, :], g.mask4[:, :], float(T) / LM, None, ALU.mult)
            dve.wait_ge(sem("w_loaded"), 16 * 10)
            for c in range(3):
                nc.vector.tensor_copy(g.wqkv0[:, c, :], raw[:, :].rearrange("p (n c) -> p n c", c=3)[:, :, c])
            nc.vector.tensor_scalar(g.cols[:, 4:6], g.cols[:, 2:4], -1.0, 1.0, ALU.mult, ALU.add)
            dve.wait_ge(sem("wT_ready"), 1)
            for i, dst in enumerate((g.wrT, g.wkT, g.wvT)):
                nc.vector.tensor_copy(dst[:, :], g.ps[:, i * P:(i + 1) * P])
            nc.vector.tensor_copy(g.wgT[:, :], g.ps[:, 3 * P:3 * P + E])
            nc.vector.tensor_copy(g.b1T[:, :], g.bank(1)[:, 0:E * HC])
            g.dve_steps = link.n

        @block.tensor
        def _(pe):
            pe.wait_ge(sem("ident_set"), 1)
            pe.wait_ge(sem("w_loaded"), 16 * 10)
            for i in range(3):
                nc.tensor.transpose(g.ps[:, i * P:(i + 1) * P], wrkv[:, i, :], g.ident[:, :])
            nc.tensor.transpose(g.ps[:, 3 * P:3 * P + E], wg[:, :], g.ident[0:E, 0:E])
            nc.tensor.transpose(g.bank(1)[:, 0:E * HC], b1raw[:, :], g.ident[0:E * HC, 0:E * HC])\
              .then_inc(sem("wT_ready"), 1)


def rows_times(nc, dst, lhs, rhs):
    n = rhs.shape[1]
    for t in range(TB):
        last = nc.tensor.matmul(dst[:, t * n:(t + 1) * n], lhs[:, t * P:(t + 1) * P], rhs, start=True, stop=True)
    return last


def wide(nc, dst, lhs, rhs):
    for j in range(T // BANK):
        last = nc.tensor.matmul(dst[:, j * BANK:(j + 1) * BANK], lhs, rhs[:, j * BANK:(j + 1) * BANK],
                                start=True, stop=True)
    return last


def fold(link, nc, tmp, dst, src, op):
    n = src.shape[1]
    link(nc.gpsimd.tensor_tensor(tmp[:, 0:n, 0:4], src[:, :, 0:4], src[:, :, 4:8], op))
    link(nc.gpsimd.tensor_tensor(tmp[:, 0:n, 4:6], tmp[:, 0:n, 0:2], tmp[:, 0:n, 2:4], op))
    link(nc.gpsimd.tensor_tensor(dst.unsqueeze(2), tmp[:, 0:n, 4:5], tmp[:, 0:n, 5:6], op))


ITERS = 6
GR = 4
NG = NPAIR // GR
WIDE = P // HD


def layer0_inputs(g):
    nc, sem = g.nc, g.sem
    with ExitStack() as mem:
        sb = lambda name, shape, dt=F32: mem.enter_context(nc.sbuf_tensor(name, shape, dt))
        sm = sb("a_small", [P, 8, TB])
        xc = sb("a_xc", [P, TB, D])
        sq = sb("a_sq", [P, TB, D])
        xnb = sb("a_xnb", [P, TB, D])
        znb = sb("a_znb", [P, TB, D])
        xnT = sb("a_xnT", [P, T + 1])
        znT = sb("a_znT", [P, T])
        xrT = sb("a_xrT", [P, T])
        xkT = sb("a_xkT", [P, T])
        tmp = sb("a_tmp", [P, T])
        tmp2 = sb("a_tmp2", [P, T])
        res = [sb(f"a_res{c}", [P, T]) for c in "qk"]
        part = [[sb(f"a_{c}{i}", [P, T], BF16) for i in range(NPART)] for c in "qk"]
        vs = sb("a_vs", [P, H, TB, 2 * HD])
        rg = sb("a_rg", [P, T])
        ka = sb("a_ka", [P, T])
        kaT = sb("a_kaT", [P, T])
        pr = sb("a_pr", [P, T])
        sg = sb("a_sg", [P, T])
    D0, D1, D2, D3 = (g.bank(2 * i, 2) for i in range(4))
    tiles = lambda ap: ap.rearrange("p (n c) -> p n c", c=P)
    s8, mu8, ss8, v8, rstd8, t8, v28, r28 = (sm[:, i, :] for i in range(8))
    NORM_LINKS = 7

    def all_batches(eng, batch):
        batch(0, False, True)
        with eng.Fori(1, B - 1) as b:
            batch(b, True, True)
        batch(B - 1, True, False)

    with nc.Block() as block:

        @block.vector
        def _(dve):
            def norm(n, part, before=True):
                link = Link(dve, sem("a_norm"), n, NORM_LINKS, (0, 3, 5, 7)[part])
                x = g.X[:, bass.ds(n * TB, TB), :]
                if part == 0:
                    link(nc.vector.reduce_sum(s8, x, AX.X))
                    link(nc.vector.tensor_scalar(mu8, s8, 1.0 / D, None, ALU.mult))
                    link(nc.vector.tensor_tensor(xc[:, :, :], x, over_last(mu8, D), ALU.subtract))
                elif part == 1:
                    link(nc.vector.tensor_tensor(sq[:, :, :], xc[:, :, :], xc[:, :, :], ALU.mult))
                    link(nc.vector.reduce_sum(ss8, sq[:, :, :], AX.X))
                    nc.vector.tensor_scalar(v8, ss8, 1.0 / D, EPS, ALU.mult, ALU.add).then_inc(sem("a_var"), 1)
                elif part == 2:
                    if before:
                        dve.wait_ge(sem("a_T_ps"), n * 2)
                        dve.wait_ge(sem("a_xn_kept"), n)
                    dve.wait_ge(sem("a_rstd"), at(n, 2, 1))
                    nc.vector.tensor_tensor(xnb[:, :, :], xc[:, :, :], over_last(rstd8, D), ALU.mult)\
                      .then_inc(sem("a_xn"), 1)
                    link(nc.vector.tensor_tensor(t8, rstd8, rstd8, ALU.mult))
                    link(nc.vector.tensor_tensor(t8, t8, ss8, ALU.mult))
                    nc.vector.tensor_scalar(v28, t8, 1.0 / D, EPS, ALU.mult, ALU.add).then_inc(sem("a_var"), 1)
                else:
                    dve.wait_ge(sem("a_rstd"), at(n, 2, 2))
                    dve.wait_ge(sem("a_xn"), at(n, 1, 1))
                    nc.vector.tensor_tensor(znb[:, :, :], xnb[:, :, :], over_last(r28, D), ALU.mult)\
                      .then_inc(sem("a_zn"), 1)

            def batch(b, before, more):
                link = Link(dve, sem("a_dve"), b, 2)
                dve.wait_ge(sem("a_xnT"), at(b, 1, 1))
                for j, dst in enumerate((xrT, xkT)):
                    link(nc.vector.tensor_scalar(tmp[:, :], xnT[:, 0:T], g.cols[:, 4 + j:5 + j], None, ALU.mult))
                    nc.vector.scalar_tensor_tensor(dst[:, :], xnT[:, 1:T + 1], g.cols[:, 2 + j:3 + j], tmp[:, :],
                                                   ALU.mult, ALU.add).then_inc(sem("a_shifted"), 1)
                    dve.wait_ge(sem("a_shifted"), at(b, 2, j + 1))
                for j, src in enumerate((D2, D3)):
                    dve.wait_ge(sem("a_part1"), at(b, 2, j + 1))
                    nc.vector.tensor_tensor(res[j][:, :], src, part[j][0][:, :], ALU.subtract)\
                      .then_inc(sem("a_res"), 1)
                if more:
                    norm(b + 1, 0)
                for j in range(2):
                    dve.wait_ge(sem("a_part2"), at(b, 2, j + 1))
                    if before and j == 0:
                        dve.wait_ge(sem("a_stored2"), b * (16 * 2 * NPART))
                    nc.vector.tensor_tensor(part[j][2][:, :], res[j][:, :], part[j][1][:, :], ALU.subtract)\
                      .then_inc(sem("a_part3"), 1)
                if more:
                    norm(b + 1, 1)
                dve.wait_ge(sem("a_relu"), at(b, 1, 1))
                nc.vector.tensor_tensor(kaT[:, :], ka[:, :], ka[:, :], ALU.mult).then_inc(sem("a_kact"), 1)
                if more:
                    norm(b + 1, 2)
                dve.wait_ge(sem("a_sigr"), at(b, 1, 1))
                dve.wait_ge(sem("a_kv"), at(b, 1, 1))
                if before:
                    dve.wait_ge(sem("a_gate"), b)
                nc.vector.tensor_tensor(pr[:, :], rg[:, :], D3, ALU.mult).then_inc(sem("a_prod"), 1)
                if more:
                    norm(b + 1, 3)
                dve.wait_ge(sem("a_prod"), at(b, 1, 1))
                dve.wait_ge(sem("a_sigp"), at(b, 1, 1))
                nc.vector.tensor_tensor(g.G[:, bass.ds(b * TB, TB), :], tiles(pr[:, :]), tiles(sg[:, :]), ALU.mult)\
                  .then_inc(sem("a_gate"), 1)
                link.end()

            for part_ in range(4):
                norm(0, part_, before=False)
            nc.vector.memset(xnT[:, 0:1], 0.0).then_inc(sem("a_const"), 1)
            dve.wait_ge(sem("a_const"), 2)
            all_batches(dve, batch)

        @block.gpsimd
        def _(pool):
            nc.gpsimd.memset(vs[:, :, :, HD:2 * HD], 1.0).then_inc(sem("a_const"), 1)
            with pool.Fori(0, B) as b:
                pool.wait_ge(sem("a_var"), at(b, 2, 1))
                nc.gpsimd.tensor_tensor(rstd8, v8, g.eps_pow[:, :], ALU.pow).then_inc(sem("a_rstd"), 1)
                pool.wait_ge(sem("a_var"), at(b, 2, 2))
                nc.gpsimd.tensor_tensor(r28, v28, g.eps_pow[:, :], ALU.pow).then_inc(sem("a_rstd"), 1)
                pool.wait_ge(sem("a_xn"), at(b, 1, 1))
                nc.gpsimd.tensor_tensor(g.XN[:, bass.ds(b * TB, TB), :], xnb[:, :, :],
                                        g.bproj[:, :].unsqueeze(1).broadcast_to([P, TB, D]), ALU.add)\
                  .then_inc(sem("a_xn_kept"), 1)

        @block.scalar
        def _(act):
            def batch(b, before, more):
                act.wait_ge(sem("a_T_ps"), at(b, 2, 1))
                act.activation(xnT[:, 1:T + 1], D0, ACT.Copy).then_inc(sem("a_xnT"), 1)
                act.wait_ge(sem("a_T_ps"), at(b, 2, 2))
                act.activation(znT[:, :], D1, ACT.Identity, bias=g.cols[:, 1:2], scale=g.cols[:, 0:1])\
                   .then_inc(sem("a_znT"), 1)
                for j, src in enumerate((D2, D3)):
                    if before and j == 0:
                        act.wait_ge(sem("a_stored0"), b * (16 * 2 * NPART))
                    act.wait_ge(sem("a_qk"), at(b, 2, j + 1))
                    act.activation(part[j][0][:, :], src, ACT.Copy).then_inc(sem("a_part1"), 1)
                if before:
                    act.wait_ge(sem("a_stored1"), b * (16 * 2 * NPART))
                for j in range(2):
                    act.wait_ge(sem("a_res"), at(b, 2, j + 1))
                    act.activation(part[j][1][:, :], res[j][:, :], ACT.Copy).then_inc(sem("a_part2"), 1)
                act.wait_ge(sem("a_kk"), at(b, 1, 1))
                act.activation(ka[:, :], D2, ACT.Relu).then_inc(sem("a_relu"), 1)
                act.wait_ge(sem("a_v"), at(b, 1, 1))
                if before:
                    act.wait_ge(sem("a_v_stored"), b * 16)
                act.activation(vs[:, :, :, 0:HD].rearrange("p h n d -> p n h d"),
                               D0.rearrange("p (n h d) -> p n h d", h=H, d=HD), ACT.Copy).then_inc(sem("a_vs"), 1)
                act.wait_ge(sem("a_r"), at(b, 1, 1))
                act.activation(rg[:, :], D1, ACT.Sigmoid).then_inc(sem("a_sigr"), 1)
                act.wait_ge(sem("a_prod"), at(b, 1, 1))
                act.activation(sg[:, :], pr[:, :], ACT.Sigmoid).then_inc(sem("a_sigp"), 1)

            all_batches(act, batch)

        @block.tensor
        def _(pe):
            def transposes(n, before=True):
                for dst, src, ready, out in ((D0, xnb, "a_xn", "a_vs"), (D1, znb, "a_zn", "a_sigr")):
                    pe.wait_ge(sem(ready), at(n, 1, 1))
                    if before:
                        pe.wait_ge(sem(out), n)
                    for t in range(TB):
                        last = nc.tensor.transpose(dst[:, t * P:(t + 1) * P], src[:, t, :], g.ident[:, :])
                    last.then_inc(sem("a_T_ps"), 1)

            def batch(b, before, more):
                pe.wait_ge(sem("a_znT"), at(b, 1, 1))
                wide(nc, D2, g.wqkv0[:, 0, :], znT[:, :]).then_inc(sem("a_qk"), 1)
                if before:
                    pe.wait_ge(sem("a_prod"), b)
                wide(nc, D3, g.wqkv0[:, 1, :], znT[:, :]).then_inc(sem("a_qk"), 1)
                pe.wait_ge(sem("a_xnT"), at(b, 1, 1))
                rows_times(nc, D0, znT, g.wqkv0[:, 2, :]).then_inc(sem("a_v"), 1)
                pe.wait_ge(sem("a_shifted"), at(b, 2, 2))
                pe.wait_ge(sem("a_res"), at(b, 2, 1))
                wide(nc, D2, g.wkT[:, :], xkT[:, :]).then_inc(sem("a_kk"), 1)
                rows_times(nc, D1, xrT, g.wrT[:, :]).then_inc(sem("a_r"), 1)
                pe.wait_ge(sem("a_kact"), at(b, 1, 1))
                pe.wait_ge(sem("a_res"), at(b, 2, 2))
                rows_times(nc, D3, kaT, g.wvT[:, :]).then_inc(sem("a_kv"), 1)
                if more:
                    transposes(b + 1)

            transposes(0, before=False)
            all_batches(pe, batch)

        @block.sync
        def _(sp):
            def batch(b, before, more):
                for i in range(NPART):
                    sp.wait_ge(sem(f"a_part{i + 1}"), at(b, 2, 2))
                    for j, ops in enumerate((g.q_ops, g.k_ops)):
                        for m in range(NPART):
                            r = NPART * i + m if j == 0 else NPART * m + i
                            dst = ops[bass.ds(b * (H // HQ), H // HQ), :, r * HD:(r + 1) * HD, :]
                            sp.dma_start(dst.rearrange("q h d t -> (q h) d t"), part[j][i][:, :])\
                              .then_inc(sem(f"a_stored{i}"), 16)
                sp.wait_ge(sem("a_vs"), at(b, 1, 1))
                sp.wait_ge(sem("a_const"), 2)
                sp.dma_start(g.v_ops[bass.ds(b * (H // HQ), H // HQ), :, :, :].rearrange("q p h n -> p q h n"),
                             vs[:, :, :, :].rearrange("p (q h) n c -> p q h (n c)", q=H // HQ))\
                  .then_inc(sem("a_v_stored"), 16)

            all_batches(sp, batch)
            for i in range(NPART):
                sp.wait_ge(sem(f"a_stored{i}"), 16 * 2 * NPART * B)
            sp.wait_ge(sem("a_v_stored"), 16 * B)


SLOTS = 3
UNITS = 32
GROUPS = UNITS // 2
MAXES = 64
ITEMS = MAXES + 1
LATE = 4
LEAD = 8
MAX_BANKS = 3
E_RING = 6


def layer0_attention(g):
    nc, sem = g.nc, g.sem
    with ExitStack() as mem:
        sb = lambda name, shape, dt=F32: mem.enter_context(nc.sbuf_tensor(name, shape, dt))
        q = [sb(f"b_q{c}", [KROWS, HQ, T], BF16) for c in range(SLOTS)]
        k = [sb(f"b_k{c}", [KROWS, HQ, T], BF16) for c in range(SLOTS)]
        v = [sb(f"b_v{c}", [P, HQ * P + 2 * HD]) for c in range(SLOTS)]
        ex = sb("b_exp_ring", [P, E_RING, 2, BANK])
        acc = sb("b_acc", [P, 2, BANK])
        mx = sb("b_mx", [P, MAXES])
        m = sb("b_m", [P, HQ * TB])
        credit = sb("b_credit", [P, 6])
        neg_rest = sb("b_neg_rest", [HQ * TB, P])
        neg = sb("b_neg", [HQ * TB, NPART, P], BF16)
        zeros = sb("b_zeros", [E * 5, 2048])
    AV = g.bank(3)
    LOOPED = QUADS // SLOTS - 1
    val = lambda j, per, c, n: j * (SLOTS * per) + (c * per + n)
    last_quad = lambda j, c: isinstance(j, int) and j * SLOTS + c == QUADS - 1
    beyond = lambda j, c: isinstance(j, int) and j * SLOTS + c >= QUADS
    through = lambda u: ITEMS + (u + 1 + LEAD) * ITEMS // UNITS

    def items(j, c, lo, hi):
        for n in range(lo, hi):
            cc, i = c + n // ITEMS, n % ITEMS
            if beyond(j, cc):
                if not beyond(j, cc - 1) and i == 0:
                    yield ITEMS * cc, cc - 1, None
            elif i == LATE:
                if not (isinstance(j, int) and j * SLOTS + cc == 0):
                    yield ITEMS * cc + i, cc - 1, None
            else:
                yield ITEMS * cc + i, cc, i - (i > LATE)

    with nc.Block() as block:

        @block.vector
        def _(dve):
            for c in range(SLOTS):
                nc.vector.memset(q[c][64:KROWS, :, :].rearrange("p h t -> p (h t)").bitcast(F32), 0.0)
                nc.vector.memset(k[c][64:KROWS, :, :].rearrange("p h t -> p (h t)").bitcast(F32), 1.0 + 0x3F80 / 2 ** 23)
                nc.vector.memset(v[c][:, HQ * P:], 0.0).then_inc(sem("b_rows_set"), 1)
            nc.vector.memset(credit[:, 4:5], 0.0).then_inc(sem("b_exp_done"), 2)

            def item(j, n, c, block):
                count = j * (SLOTS * ITEMS) + (n + 1)
                bank = g.bank(n % MAX_BANKS)
                dve.wait_ge(sem("b_max_scores"), count)
                if block is not None:
                    if (n % ITEMS, block) == (LATE + 1, LATE) and isinstance(j, int) and j * SLOTS + c == 0:
                        nc.vector.memset(credit[:, 5:6], 0.0).then_inc(sem("b_max_done"), 1)
                    nc.vector.reduce_max(mx[:, block:block + 1], bank, AX.X)\
                      .then_inc(sem("b_max_done"), 1)
                    if block == MAXES - 1:
                        dve.wait_ge(sem("b_max_done"), count)
                        nc.vector.reduce_max(m[:, :],
                                             mx[:, :].rearrange("p (n a) -> p n a", a=2), AX.X)\
                          .then_inc(sem("b_m"), 1)
                        dve.wait_ge(sem("b_m"), val(j, 1, c, 1))
                    return
                mT = bank[0:HQ * TB, 0:P]
                if not (isinstance(j, int) and j * SLOTS + c == 0):
                    dve.wait_ge(sem("b_m_loaded"), val(j, 16 * NPART, c, 0))
                link = Link(dve, sem("b_dve"), j, 3 * SLOTS, 3 * c)
                link(nc.vector.tensor_scalar(neg[:, 0, :], mT, -1.0, None, ALU.mult))
                link(nc.vector.scalar_tensor_tensor(neg_rest[:, :], mT, -1.0, neg[:, 0, :], ALU.mult, ALU.subtract))
                link(nc.vector.tensor_copy(neg[:, 1, :], neg_rest[:, :]))
                nc.vector.tensor_tensor(neg[:, 2, :], neg_rest[:, :], neg[:, 1, :], ALU.subtract)\
                  .then_inc(sem("b_max_done"), 1)

            for it in items(0, 0, 0, through(-1)):
                item(0, *it)
            with dve.Fori(0, LOOPED) as j:
                for c in range(SLOTS):
                    for it in items(j, c, through(-1), through(UNITS - 1)):
                        item(j, *it)
            for c in range(SLOTS + 1):
                for it in items(LOOPED, c, through(-1), through(UNITS - 1)):
                    item(LOOPED, *it)

        @block.scalar
        def _(act):
            def evacuate(j, half):
                act.wait_ge(sem("b_av"), val(j, GROUPS, 0, TB * (half + 1) + 3))
                s = half % 2
                act.wait_ge(sem(f"b_stored{s}"), val(j, 16 * HQ, 0, 16 * HQ * (half // 2 + 1)))
                act.activation(acc[:, s, :], AV, ACT.Copy).then_inc(sem("b_acc"), 1)

            def quad(j, c, carry, flush):
                for u in range(UNITS):
                    n = UNITS * c + u
                    act.wait_ge(sem("b_scores"), val(j, UNITS, 0, n + 1))
                    act.wait_ge(sem("b_av"), val(j, GROUPS, 0, n // 2 + 1))
                    b = 4 + 2 * (u % 2)
                    act.activation(ex[:, n % E_RING, :, :], g.bank(b, 2).rearrange("p (h t) -> p h t", h=2),
                                   ACT.Exp, scale=ATT_SCALE).then_inc(sem("b_exp_done"), 1)
                    if u == 2 and carry:
                        evacuate(j, 2 * c - 1)
                    if u == 18:
                        evacuate(j, 2 * c)
                if flush:
                    evacuate(j, 2 * c + 1)

            with act.Fori(0, LOOPED) as j:
                for c in range(SLOTS):
                    quad(j, c, c > 0, c == SLOTS - 1)
            for c in range(SLOTS + 1):
                quad(LOOPED, c, c > 0, c == SLOTS)

        @block.tensor
        def _(pe):
            def item(j, n, c, block):
                s = c % SLOTS
                if block == 0:
                    pe.wait_ge(sem(f"b_loaded{s}"), val(j, 16, 0, 48 * (c // SLOTS + 1)))
                if not (isinstance(j, int) and j == 0 and n < MAX_BANKS):
                    pe.wait_ge(sem("b_max_done"), j * (SLOTS * ITEMS) + (n - MAX_BANKS + 1))
                if block is None:
                    pe.wait_ge(sem("b_m"), val(j, 1, c, 1))
                    nc.tensor.transpose(g.bank(n % MAX_BANKS)[0:HQ * TB, 0:P], m[:, :], g.ident[:, :])\
                      .then_inc(sem("b_max_scores"), 1)
                    return
                h, t, half = block // 16, block // 2 % TB, block % 2
                counts = 2 if isinstance(j, int) and j * SLOTS + c == 0 and block == LATE - 1 else 1
                nc.tensor.matmul(g.bank(n % MAX_BANKS), q[s][:, h, t * P:(t + 1) * P],
                                 k[s][:, h, half * BANK:(half + 1) * BANK], start=True, stop=True)\
                  .then_inc(sem("b_max_scores"), counts)

            def times_v(j, c, group):
                s, half, kb = c % SLOTS, group // TB, group % TB
                n = UNITS * c + 2 * group
                pe.wait_ge(sem("b_exp_done"), val(j, UNITS, 0, n + 2 + 2))
                if kb == 0:
                    pe.wait_ge(sem("b_acc"), val(j, 2, c, half + 1))
                for h in range(HQ):
                    e = ex[:, (n + h // 2) % E_RING, h % 2, :]
                    last = nc.tensor.matmul(g.ps[32 * h:32 * h + 32, 3 * BANK:4 * BANK],
                                            v[s][:, h * P + kb * 2 * HD:h * P + kb * 2 * HD + 32], e,
                                            start=(kb == 0), stop=(kb == TB - 1))
                last.then_inc(sem("b_av"), 1)

            def quad(j, c, carry, flush):
                s = c % SLOTS
                for u in range(UNITS):
                    n = UNITS * c + u
                    half, kb, pair = u // 16, u // 2 % TB, u % 2
                    if u == 0:
                        pe.wait_ge(sem("b_m_loaded"), val(j, 16 * NPART, c, 16 * NPART))
                    todo = list(items(j, c, through(u - 1), through(u)))
                    pe.wait_ge(sem("b_exp_done"), val(j, UNITS, 0, n + 1))
                    for i in range(2):
                        h = 2 * pair + i
                        last = nc.tensor.matmul(g.bank(4 + 2 * (u % 2) + i), k[s][:, h, kb * P:(kb + 1) * P],
                                                q[s][:, h, half * BANK:(half + 1) * BANK], start=True, stop=True)
                    last.then_inc(sem("b_scores"), 1)
                    for it in todo[:1]:
                        item(j, *it)
                    if u == 1 and carry:
                        times_v(j, c - 1, GROUPS - 1)
                    if u >= 3 and u % 2:
                        times_v(j, c, (u - 3) // 2)
                    for it in todo[1:]:
                        item(j, *it)
                if flush:
                    times_v(j, c, GROUPS - 1)

            pe.wait_ge(sem("b_rows_set"), SLOTS)
            for it in items(0, 0, 0, through(-1)):
                item(0, *it)
            with pe.Fori(0, LOOPED) as j:
                for c in range(SLOTS):
                    quad(j, c, c > 0, c == SLOTS - 1)
            for c in range(SLOTS + 1):
                quad(LOOPED, c, c > 0, c == SLOTS)

        @block.gpsimd
        def _(pool):
            nc.gpsimd.memset(credit[:, 0:1], 0.0).then_inc(sem("b_av"), 3)
            nc.gpsimd.memset(credit[:, 1:2], 0.0).then_inc(sem("b_acc"), 1)
            for s in range(2):
                nc.gpsimd.memset(credit[:, 2 + s:3 + s], 0.0).then_inc(sem(f"b_stored{s}"), 16 * HQ)
            nc.gpsimd.memset(zeros[:, :], 0.0).then_inc(sem("b_zeros"), 1)

        @block.sync
        def _(sp):
            def load(quad, c):
                one = bass.ds(quad, 1)
                sp.dma_start(q[c][0:ROWS + NPART, :, :], g.q_ops[one, :, :, :].rearrange("a h r t -> (a r) h t"))\
                  .then_inc(sem(f"b_loaded{c}"), 16)
                sp.dma_start(k[c][0:ROWS, :, :], g.k_ops[one, :, :, :].rearrange("a h r t -> (a r) h t"))\
                  .then_inc(sem(f"b_loaded{c}"), 16)
                sp.dma_start(v[c][:, 0:HQ * P], g.v_ops[one, :, :, :].rearrange("a p h n -> (a p) (h n)"))\
                  .then_inc(sem(f"b_loaded{c}"), 16)

            def store_maxima(j, c):
                n = ITEMS * (c + 1) + (1 if last_quad(j, c) else LATE + 1)
                sp.wait_ge(sem("b_max_done"), j * (SLOTS * ITEMS) + n)
                for i in range(NPART):
                    dst = q[c % SLOTS][ROWS + i:ROWS + i + 1, :, :].rearrange("r h (t x) -> r (h t) x", x=P)
                    sp.dma_start(dst, neg[:, i, :]).then_inc(sem("b_m_loaded"), 16)

            def store_half(j, c, half):
                sp.wait_ge(sem("b_acc"), val(j, 2, c, half + 1 + 1))
                for h in range(HQ):
                    dst = g.av_out[bass.ds(j * SLOTS + c, 1), h, :, half * BANK:(half + 1) * BANK]
                    sp.dma_start(dst.rearrange("a r t -> (a r) t"), acc[32 * h:32 * h + 2 * HD, half, :])\
                      .then_inc(sem(f"b_stored{half}"), 16)

            def quad(j, c):
                store_half(j, c, 0)
                if not last_quad(j, c):
                    store_maxima(j, c + 1)
                store_half(j, c, 1)
                if not beyond(j, c + SLOTS):
                    sp.wait_ge(sem("b_av"), val(j, GROUPS, c, GROUPS + 3))
                    load(j * SLOTS + (c + SLOTS), c)

            for c in range(SLOTS):
                sp.wait_ge(sem("b_rows_set"), c + 1)
                load(c, c)
                if c == 0:
                    sp.wait_ge(sem("b_loaded0"), 16 * 3)
            store_maxima(0, 0)
            sp.wait_ge(sem("b_zeros"), 1)
            flat = g.x_disp[0:E * CAP, :].rearrange("(q r) d -> q (r d)", q=E * 5)
            for i in range(0, CAP * D // 5, 2048):
                n = min(2048, CAP * D // 5 - i)
                sp.dma_start(flat[:, i:i + n], zeros[:, 0:n]).then_inc(sem("disp_zeroed"), 16)
            with sp.Fori(0, LOOPED) as j:
                for c in range(SLOTS):
                    quad(j, c)
            for c in range(SLOTS + 1):
                quad(LOOPED, c)
            for s in range(2):
                sp.wait_ge(sem(f"b_stored{s}"), 16 * HQ * (QUADS + 1))
            sp.wait_ge(sem("disp_zeroed"), 16 * -(-(CAP * D // 5) // 2048))


def heads_of(ap, mask, n):
    return ap.unsqueeze(1).broadcast_to([P, H, n]), over_last(mask, n)


def layer0_outputs(g):
    nc, sem = g.nc, g.sem
    g.LG = g.sb("logits", [P, NT, E])
    g.KS = g.sb("k_softmax", [P, NPAIR, LM])
    g.KB = g.sb("k_blocks", [P, NPAIR, P])
    g.NV = g.sb("nv", [P, NPAIR + WIDE, HD])
    g.KL = g.sb("kl_sums", [P, B, LM])
    g.CW = g.sb("choice_weight", [P, TOPK, NT])
    g.gates = g.sb("r_gates", [P, NT, E])
    g.gx = g.sb("r_gx", [P, NT, E])
    g.oh = g.sb("r_onehot", [P, TOPK, NT, E])
    g.rsum = g.sb("r_sum", [P, NT])
    g.fold = g.sb("r_fold", [P, TOPK * NT, 6])
    g.idx = g.sb("r_idx", [P, TOPK, NT])
    g.upper = g.sb("r_upper", [P, P])
    g.ones = g.sb("r_ones", [P, P])
    g.iint = g.sb("r_iota_int", [P, E + TOPK * NT], I32)
    g.iof = g.sb("r_iota", [P, E + TOPK * NT])
    with ExitStack() as mem:
        sb = lambda name, shape, dt=F32: mem.enter_context(nc.sbuf_tensor(name, shape, dt))
        dens = sb("c_dens", [P, B, P])
        num = sb("c_num", [P, T])
        den = sb("c_den", [P, T])
        oT = sb("c_oT", [P, T])
        sm = sb("c_small", [P, 8, TB])
        t1 = sb("c_t1", [P, TB, D])
        xb = sb("c_xb", [P, TB, D])
        xc = sb("c_xc", [P, TB, D])
        xnb = sb("c_xnb", [P, TB, D])
        xT = sb("c_xT", [P, T])
        qT = sb("c_qT", [P, T])
        kT = sb("c_kT", [P, T])
        v1 = sb("c_v1", [P, TB, D])
        qsum = sb("c_qsum", [P, LM])
        kl = sb("c_kl", [P, LM])
        qlm = sb("c_qlm", [P, H, LM])
        kx = sb("c_kx", [P, PAIRS, LM])
        ke = sb("c_ke", [P, PAIRS, LM])
        en = sb("c_en", [P, 2, T])
        enT = sb("c_enT", [P, TB, H * LM])
        nvT = sb("c_nvT", [P, 4, LM])
        nm = sb("c_nm", [P, PAIRS])
        nden = sb("c_nden", [P, PAIRS])
        nrec = sb("c_nrec", [P, PAIRS])
        credit = sb("c_credit", [P, 2])
    D0, D1, D2, D3 = (g.bank(2 * i, 2) for i in range(4))
    s8, mu8, ss8, v8, rstd8, kmx, ksum, krec = (sm[:, i, :] for i in range(8))
    tiles = lambda ap: ap.rearrange("p (n c) -> p n c", c=P)
    KPS = g.ps[:, 0:PAIRS * LM].rearrange("p (n c) -> p n c", c=LM)
    LGPS = g.bank(1)[:, 0:TB * E]
    NVPS = g.ps[:, 0:4 * LM].rearrange("p (i n) -> p i n", i=4)
    NORM_LINKS = 6

    with nc.Block() as block:

        @block.vector
        def _(dve):
            def router(part):
                link = Link(dve, sem("dve_step"), start=g.dve_steps)
                iota8 = g.iof[:, 0:E].unsqueeze(1).broadcast_to([P, NT, E])
                spread = lambda ap: over_last(ap, E)
                gates, gx, oh, idx, rsum = g.gates, g.gx, g.oh, g.idx, g.rsum
                if part == 0:
                    dve.wait_ge(sem("c_lg_kept"), B)
                    link(nc.vector.reduce_max(rsum[:, :], g.LG[:, :, :], AX.X))
                    nc.vector.tensor_tensor(gx[:, :, :], g.LG[:, :, :], spread(rsum[:, :]), ALU.subtract)\
                      .then_inc(sem("r_gx"), 1)
                elif part == 1:
                    dve.wait_ge(sem("r_exp"), 1)
                    dve.wait_ge(sem("r_iota"), 1)
                    link(nc.vector.reduce_sum(rsum[:, :], gates[:, :, :], AX.X))
                    link(nc.vector.reciprocal(rsum[:, :], rsum[:, :]))
                    link(nc.vector.tensor_tensor(gates[:, :, :], gates[:, :, :], spread(rsum[:, :]), ALU.mult))
                elif part % 2 == 0:
                    k = (part - 2) // 2
                    link(nc.vector.reduce_max(g.CW[:, k, :], gates[:, :, :], AX.X))
                    link(nc.vector.tensor_tensor(gx[:, :, :], gates[:, :, :], spread(g.CW[:, k, :]), ALU.is_equal))
                    link(nc.vector.tensor_tensor(gx[:, :, :], gx[:, :, :], iota8, ALU.mult))
                else:
                    k = (part - 3) // 2
                    link(nc.vector.tensor_reduce(idx[:, k, :], gx[:, :, :], AX.X, ALU.min))
                    link(nc.vector.tensor_tensor(oh[:, k, :, :], iota8, spread(idx[:, k, :]), ALU.is_equal))
                    if k == 0:
                        link(nc.vector.scalar_tensor_tensor(gates[:, :, :], oh[:, k, :, :], -2.0, gates[:, :, :],
                                                            ALU.mult, ALU.add))
                g.dve_steps = link.n

            def divide(n):
                dve.wait_ge(sem("c_av"), at(n, 32, 32))
                nc.vector.tensor_tensor(oT[:, :], num[:, :], den[:, :], ALU.mult).then_inc(sem("c_oT"), 1)

            def norm(n, part):
                mine = bass.ds(n * TB, TB)
                link = Link(dve, sem("c_norm"), n, NORM_LINKS, (0, 0, 1, 4, 5, 6)[part])
                if part == 0:
                    dve.wait_ge(sem("c_s"), at(n, 1, 1))
                    nc.vector.tensor_tensor(t1[:, :, :], tiles(D0), g.XN[:, mine, :], ALU.add).then_inc(sem("c_t1"), 1)
                    dve.wait_ge(sem("c_t1"), at(n, 1, 1))
                if part == 1:
                    link(nc.vector.tensor_tensor(t1[:, :, :], t1[:, :, :], g.G[:, mine, :], ALU.mult))
                    if not isinstance(n, int):
                        dve.wait_ge(sem("c_x_kept"), n)
                    nc.vector.tensor_tensor(xb[:, :, :], g.X[:, mine, :], t1[:, :, :], ALU.add).then_inc(sem("c_x"), 1)
                    dve.wait_ge(sem("c_x"), at(n, 1, 1))
                if part == 2:
                    link(nc.vector.reduce_sum(s8, xb[:, :, :], AX.X))
                    link(nc.vector.tensor_scalar(mu8, s8, 1.0 / D, None, ALU.mult))
                    link(nc.vector.tensor_tensor(xc[:, :, :], xb[:, :, :], over_last(mu8, D), ALU.subtract))
                if part == 3:
                    link(nc.vector.tensor_tensor(t1[:, :, :], xc[:, :, :], xc[:, :, :], ALU.mult))
                if part == 4:
                    link(nc.vector.reduce_sum(ss8, t1[:, :, :], AX.X))
                    nc.vector.tensor_scalar(v8, ss8, 1.0 / D, EPS, ALU.mult, ALU.add).then_inc(sem("c_var"), 1)
                if part == 5:
                    dve.wait_ge(sem("c_rstd"), at(n, 1, 1))
                    if not isinstance(n, int):
                        dve.wait_ge(sem("c_xT_ps"), n)
                        dve.wait_ge(sem("c_xn_kept"), n)
                    nc.vector.tensor_tensor(xnb[:, :, :], xc[:, :, :], over_last(rstd8, D), ALU.mult)\
                      .then_inc(sem("c_xn"), 1)

            def batch(b, more):
                link = Link(dve, sem("c_dve"), b, 6)
                if more:
                    divide(b + 1)
                dve.wait_ge(sem("c_qT"), at(b, 1, 1))
                link(nc.vector.reduce_sum(qsum[:, :], qT[:, :].rearrange("p (n c) -> p n c", n=LM), AX.X))
                nc.vector.tensor_tensor(qlm[:, :, :], *heads_of(qsum[:, :], g.headmask[:, :], LM), ALU.mult)\
                  .then_inc(sem("c_landmarks"), 1)
                dve.wait_ge(sem("c_kT"), at(b, 1, 1))
                ksums = g.KL[:, bass.ds(b, 1), :].rearrange("p a n -> p (a n)")
                link(nc.vector.reduce_sum(ksums, kT[:, :].rearrange("p (n c) -> p n c", n=LM), AX.X))
                nc.vector.tensor_scalar(kl[:, :], ksums, float(LM) / T, None, ALU.mult).then_inc(sem("c_landmarks"), 1)
                dve.wait_ge(sem("c_K_ps"), at(b, 1, 1))
                link(nc.vector.reduce_max(kmx, KPS, AX.X))
                nc.vector.tensor_tensor(kx[:, :, :], KPS, over_last(kmx, LM), ALU.subtract).then_inc(sem("c_kx"), 1)
                for p in range(PAIRS):
                    dve.wait_ge(sem("c_n_ps"), at(b, PAIRS, p + 1))
                    nc.vector.reduce_max(nm[:, p:p + 1], (D1, D2)[p % 2], AX.X, negate=True).then_inc(sem("c_nm"), 1)
                    if p == 0:
                        dve.wait_ge(sem("c_ke"), at(b, 1, 1))
                        link(nc.vector.reduce_sum(ksum, ke[:, :, :], AX.X))
                        link(nc.vector.reciprocal(krec, ksum))
                        nc.vector.tensor_tensor(g.KS[:, bass.ds(b * PAIRS, PAIRS), :], ke[:, :, :],
                                                over_last(krec, LM), ALU.mult).then_inc(sem("c_K"), 1)
                        dve.wait_ge(sem("c_zeroed"), 2)
                        for i in range(2):
                            half = slice(LM * i, LM * i + LM)
                            nc.vector.tensor_tensor(g.KB[half, bass.ds(b * PAIRS, PAIRS), half], ke[half, :, :],
                                                    over_last(krec[half, :], LM), ALU.mult).then_inc(sem("c_K"), 1)
                    elif p < 7 and more:
                        norm(b + 1, p - 1)
                    elif p < 7:
                        router(p - 1)
                dve.wait_ge(sem("c_en"), at(b, PAIRS, PAIRS))
                link(nc.vector.reciprocal(nrec[:, :], nden[:, :]))
                dve.wait_ge(sem("c_nv"), at(b, 1, 1))
                nc.vector.tensor_tensor(nvT[:, :, :], NVPS, over_last(g.mask4[:, :], LM), ALU.mult)\
                  .then_inc(sem("c_nvT"), 1)
                dve.wait_ge(sem("c_nv_ps"), at(b, 1, 1))
                for r in range(2):
                    for i in range(2):
                        half = slice(LM * i, LM * i + LM)
                        src = g.bank(1)[half, r * P:(r + 1) * P].rearrange("p (j c) -> p j c", j=4)
                        c = (2 * r + i) * HD
                        dst = g.NV[half, bass.ds(b * PAIRS, PAIRS), :].rearrange("p (j r) d -> p j r d", r=2)
                        by = nrec[half, :].rearrange("p (j r) -> p j r", r=2)[:, :, r]
                        nc.vector.tensor_tensor(dst[:, :, r, :], src[:, :, c:c + HD],
                                                by.unsqueeze(2).broadcast_to([LM, 4, HD]), ALU.mult)\
                          .then_inc(sem("c_nv_kept"), 1)
                link.end()

            dve.wait_ge(sem("c_dens0"), 16)
            nc.vector.reciprocal(dens[:, 0, :], dens[:, 0, :]).then_inc(sem("c_recs"), 1)
            dve.wait_ge(sem("c_dens1"), 16 * (B - 1))
            nc.vector.reciprocal(dens[:, 1:B, :], dens[:, 1:B, :]).then_inc(sem("c_recs"), 1)
            divide(0)
            for part in range(6):
                norm(0, part)
            with dve.Fori(0, B - 1) as b:
                batch(b, True)
            batch(B - 1, False)

        @block.gpsimd
        def _(pool):
            nc.gpsimd.memset(credit[:, 0:1], 0.0).then_inc(sem("c_q_kept"), 16)
            nc.gpsimd.memset(credit[:, 1:2], 0.0).then_inc(sem("c_nv_kept"), 4)

            def rstd(n):
                pool.wait_ge(sem("c_var"), at(n, 1, 1))
                nc.gpsimd.tensor_tensor(rstd8, v8, g.eps_pow[:, :], ALU.pow).then_inc(sem("c_rstd"), 1)

            rstd(0)
            nc.gpsimd.memset(g.KB[:, :, :], 0.0).then_inc(sem("c_zeroed"), 1)
            nc.gpsimd.memset(g.NV[:, NPAIR:, :], 0.0).then_inc(sem("c_zeroed"), 1)
            link = Link(pool, sem("pool_step"), start=g.pool_steps)
            link(nc.gpsimd.memset(g.upper[:, :], 1.0))
            link(nc.gpsimd.affine_select(out=g.upper[:, :], in_=g.upper[:, :], compare_op=ALU.is_gt, fill=0.0,
                                         base=0, pattern=[[1, P]], channel_multiplier=-1))
            nc.gpsimd.memset(g.ones[:, :], 1.0)
            nc.gpsimd.iota(g.iint[:, 0:E], pattern=[[1, E]], base=-E, channel_multiplier=0)
            link(nc.gpsimd.iota(g.iint[:, E:], pattern=[[P, TOPK * NT]], base=E * CAP, channel_multiplier=1))
            nc.gpsimd.tensor_copy(g.iof[:, :], g.iint[:, :]).then_inc(sem("r_iota"), 1)
            with pool.Fori(1, B) as n:
                rstd(n)
            g.pool_steps = link.n

        @block.scalar
        def _(act):
            def keep_x(n):
                act.wait_ge(sem("c_x"), at(n, 1, 1))
                act.activation(g.X[:, bass.ds(n * TB, TB), :], xb[:, :, :], ACT.Copy).then_inc(sem("c_x_kept"), 1)

            def keep_xn(n):
                act.wait_ge(sem("c_xn"), at(n, 1, 1))
                act.activation(g.XN[:, bass.ds(n * TB, TB), :], xnb[:, :, :], ACT.Copy).then_inc(sem("c_xn_kept"), 1)

            def batch(b, more):
                act.wait_ge(sem("c_xT_ps"), at(b, 1, 1))
                act.activation(xT[:, :], D0, ACT.Copy).then_inc(sem("c_xT"), 1)
                act.wait_ge(sem("c_q_ps"), at(b, 1, 1))
                act.wait_ge(sem("c_q_kept"), at(b, 16, 16))
                act.activation(qT[:, :], D1, ACT.Copy).then_inc(sem("c_qT"), 1)
                act.wait_ge(sem("c_k_ps"), at(b, 1, 1))
                act.activation(kT[:, :], D2, ACT.Copy).then_inc(sem("c_kT"), 1)
                act.wait_ge(sem("c_v_ps"), at(b, 1, 1))
                act.activation(v1[:, :, :], tiles(D3), ACT.Copy).then_inc(sem("c_v"), 1)
                act.wait_ge(sem("c_lg"), at(b, 1, 1))
                act.activation(g.LG[:, bass.ds(b * TB, TB), :], LGPS.rearrange("p (n e) -> p n e", e=E), ACT.Copy)\
                   .then_inc(sem("c_lg_kept"), 1)
                act.wait_ge(sem("c_kx"), at(b, 1, 1))
                act.activation(ke[:, :, :], kx[:, :, :], ACT.Exp).then_inc(sem("c_ke"), 1)

                def transposed_out(p):
                    act.wait_ge(sem("c_enT_ps"), at(b, PAIRS, p + 1))
                    act.activation(enT[:, :, p * P:(p + 1) * P], tiles(D3), ACT.Copy).then_inc(sem("c_enT"), 1)

                for p in range(PAIRS):
                    act.wait_ge(sem("c_nm"), at(b, PAIRS, p + 1))
                    if p >= 2:
                        act.wait_ge(sem("c_enT_ps"), at(b, PAIRS, p - 1))
                    act.activation(en[:, p % 2, :], (D1, D2)[p % 2], ACT.Exp, bias=nm[:, p:p + 1],
                                   accum_out=nden[:, p:p + 1]).then_inc(sem("c_en"), 1)
                    if p >= 1:
                        transposed_out(p - 1)
                    if p == 4 and more:
                        keep_x(b + 1)
                    if p == 2 and not more:
                        act.wait_ge(sem("r_gx"), 1)
                        act.activation(g.gates[:, :, :], g.gx[:, :, :], ACT.Exp).then_inc(sem("r_exp"), 1)
                transposed_out(PAIRS - 1)
                if more:
                    keep_xn(b + 1)

            keep_x(0)
            keep_xn(0)
            with act.Fori(0, B - 1) as b:
                batch(b, True)
            batch(B - 1, False)

        @block.tensor
        def _(pe):
            def project(n):
                pe.wait_ge(sem("c_oT"), at(n, 1, 1))
                rows_times(nc, D0, oT, g.wproj0[:, :]).then_inc(sem("c_s"), 1)

            def batch(b, more):
                pe.wait_ge(sem("c_xn"), at(b, 1, 1))
                pe.wait_ge(sem("c_nv_kept"), at(b, 4, 4))
                for t in range(TB):
                    last = nc.tensor.transpose(D0[:, t * P:(t + 1) * P], xnb[:, t, :], g.ident[:, :])
                last.then_inc(sem("c_xT_ps"), 1)
                pe.wait_ge(sem("c_xT"), at(b, 1, 1))
                wide(nc, D1, g.wqkv1[:, 0:P], xT[:, :]).then_inc(sem("c_q_ps"), 1)
                wide(nc, D2, g.wqkv1[:, P:2 * P], xT[:, :]).then_inc(sem("c_k_ps"), 1)
                rows_times(nc, D3, xT, g.wqkv1[:, 2 * P:3 * P]).then_inc(sem("c_v_ps"), 1)
                rows_times(nc, g.bank(1), xT, g.wgT[:, :]).then_inc(sem("c_lg"), 1)

                def n_scores(p):
                    if p >= 2:
                        pe.wait_ge(sem("c_en"), at(b, PAIRS, p - 1))
                    wide(nc, (D1, D2)[p % 2], qlm[:, 2 * p:2 * p + 2, :].rearrange("p h n -> p (h n)"), kT[:, :])\
                        .then_inc(sem("c_n_ps"), 1)

                pe.wait_ge(sem("c_landmarks"), at(b, 2, 1))
                pe.wait_ge(sem("c_kT"), at(b, 1, 1))
                n_scores(0)
                pe.wait_ge(sem("c_landmarks"), at(b, 2, 2))
                for p in range(PAIRS):
                    last = nc.tensor.matmul(KPS[:, p, :], qlm[:, 2 * p:2 * p + 2, :].rearrange("p h n -> p (h n)"),
                                            kl[:, :], start=True, stop=True)
                last.then_inc(sem("c_K_ps"), 1)
                n_scores(1)
                if more:
                    pe.wait_ge(sem("c_kx"), at(b, 1, 1))
                    pe.wait_ge(sem("c_lg_kept"), at(b, 1, 1))
                    project(b + 1)
                for p in range(PAIRS):
                    if p >= 1 and p + 1 < PAIRS:
                        n_scores(p + 1)
                    pe.wait_ge(sem("c_en"), at(b, PAIRS, p + 1))
                    pe.wait_ge(sem("c_enT"), at(b, PAIRS, p)) if p else pe.wait_ge(sem("c_v"), at(b, 1, 1))
                    for t in range(TB):
                        last = nc.tensor.transpose(D3[:, t * P:(t + 1) * P], en[:, p % 2, t * P:(t + 1) * P],
                                                   g.ident[:, :])
                    last.then_inc(sem("c_enT_ps"), 1)
                pe.wait_ge(sem("c_enT"), at(b, PAIRS, PAIRS))
                if more:
                    pe.wait_ge(sem("c_t1"), at(b + 1, 1, 1))
                else:
                    pe.wait_ge(sem("c_kx"), at(b, 1, 1))
                    pe.wait_ge(sem("c_lg_kept"), at(b, 1, 1))
                for t in range(TB):
                    for j in range(4):
                        last = nc.tensor.matmul(g.ps[32 * j:32 * j + 32, 0:4 * LM], v1[:, t, 32 * j:32 * j + 32],
                                                enT[:, t, 4 * LM * j:4 * LM * (j + 1)],
                                                start=(t == 0), stop=(t == TB - 1))
                last.then_inc(sem("c_nv"), 1)
                pe.wait_ge(sem("c_nvT"), at(b, 1, 1))
                for r in range(2):
                    last = nc.tensor.transpose(g.bank(1)[:, r * P:(r + 1) * P],
                                               nvT[:, 2 * r:2 * r + 2, :].rearrange("p i n -> p (i n)"), g.ident[:, :])
                last.then_inc(sem("c_nv_ps"), 1)

            project(0)
            with pe.Fori(0, B - 1) as b:
                batch(b, True)
            batch(B - 1, False)

        @block.sync
        def _(sp):
            def load(b):
                quads = bass.ds(b * (H // HQ), H // HQ)
                sp.dma_start(num[:, :], g.av_out[quads, :, 0:HD, :].rearrange("q h d t -> (q h) d t"))\
                  .then_inc(sem("c_av"), 16)
                src = g.recs[bass.ds(b, 1), :, :].rearrange("a h t -> (a h) t").unsqueeze(1).broadcast_to([H, HD, T])
                sp.dma_start(den[:, :], src).then_inc(sem("c_av"), 16)

            def keep_q(b):
                sp.wait_ge(sem("c_qT"), at(b, 1, 1))
                sp.dma_start(g.q1_keep[bass.ds(b, 1), :, :].rearrange("a p t -> (a p) t"), qT[:, :])\
                  .then_inc(sem("c_q_kept"), 16)

            parts = ((0, 1), (1, B))
            for i, (lo, hi) in enumerate(parts):
                for b in range(lo, hi):
                    src = g.av_out[b * 4:b * 4 + 4, :, HD, :].rearrange("q h (c t) -> (q h) c t", t=P)
                    sp.dma_start(dens[:, b, :], src).then_inc(sem(f"c_dens{i}"), 16)
            for i, (lo, hi) in enumerate(parts):
                sp.wait_ge(sem("c_recs"), i + 1)
                for b in range(lo, hi):
                    sp.dma_start(g.recs[b, :, :].rearrange("h (c t) -> h c t", t=P), dens[:, b, :])\
                      .then_inc(sem(f"c_recs_kept{i}"), 16)
                sp.wait_ge(sem(f"c_recs_kept{i}"), 16 * (hi - lo))
                if i == 0:
                    load(0)
            sp.wait_ge(sem("c_oT"), 1)
            load(1)
            with sp.Fori(0, B - 2) as b:
                keep_q(b)
                sp.wait_ge(sem("c_oT"), b + 2)
                load(b + 2)
            keep_q(B - 2)
            keep_q(B - 1)
            sp.wait_ge(sem("c_q_kept"), 16 * (B + 1))




def inverse_and_routing(g):
    nc, sem = g.nc, g.sem
    g.WM = g.sb("w_landmark", [P, NPAIR, 32])
    g.ROW = g.sb("row_taken", [P, TOPK * NT], I32)
    g.rows_out = g.sb("row_sent", [P, TOPK * NT], I32)
    kb = g.KB
    with ExitStack() as mem:
        sb = lambda name, shape, dt=F32: mem.enter_context(nc.sbuf_tensor(name, shape, dt))
        A = sb("i_a", [P, NPAIR, P])
        X = sb("i_x", [P, NPAIR, P])
        AQ = sb("i_aq", [P, NPAIR, P])
        twin = sb("i_ones", [P, P])
        eyes = sb("i_eyes", [P, 3, P])
        eye2 = sb("i_eye2", [P, LM])
        den = sb("i_den", [P, NPAIR])
        z = sb("i_z", [P, NPAIR + WIDE, HD])
        tot = sb("r_tot", [P, 4, TOPK * NT, E])
        e64 = sb("r_e64", [P, 6, TOPK * NT])
    MM0, DV, AC = NG * 3, 3 * NG, 2 * NG
    grp = lambda ap, n: ap[:, n * GR:(n + 1) * GR, :]
    bankg = lambda n: g.bank(n).rearrange("p (n c) -> p n c", c=P)
    eye = lambda i: eyes[:, i, :].unsqueeze(1).broadcast_to([P, GR, P])
    halves = [slice(LM * i, LM * i + LM) for i in range(2)]
    firsts = g.ps.rearrange("p (n c) -> p n c", c=P)[:, :, 0:HD]

    with nc.Block() as block:

        @block.gpsimd
        def _(pool):
            link = Link(pool, sem("pool_step"), start=g.pool_steps)
            nc.gpsimd.memset(z[:, NPAIR:, :], 0.0).then_inc(sem("i_wm"), 1)
            nc.gpsimd.memset(g.WM[:, :, :], 0.0).then_inc(sem("i_wm"), 1)
            pool.wait_ge(sem("r_counted"), 3)
            a, c, s = 1, 2, 1
            while s < TOPK * NT:
                link(nc.gpsimd.tensor_tensor(tot[:, c, s:, :], tot[:, a, s:, :], tot[:, a, :TOPK * NT - s, :], ALU.add))
                link(nc.gpsimd.tensor_copy(tot[:, c, :s, :], tot[:, a, :s, :]))
                a, c, s = c, a, 2 * s
            link(nc.gpsimd.tensor_tensor(tot[:, a, :, :], tot[:, a, :, :], tot[:, 0, :, :], ALU.subtract))
            link(nc.gpsimd.tensor_tensor(tot[:, c, :, :], tot[:, 3, :, :], tot[:, a, :, :], ALU.add))
            link(nc.gpsimd.tensor_tensor(tot[:, c, :, :], tot[:, c, :, :],
                                         g.oh[:, :, :, :].rearrange("p k n e -> p (k n) e"), ALU.mult))
            cnt, within, start, dump, w1, w2 = (e64[:, i, :] for i in range(6))
            flat = lambda ap: ap.rearrange("p k n -> p (k n)")
            fold(link, nc, g.fold, cnt, tot[:, c, :, :], ALU.add)
            link(nc.gpsimd.tensor_scalar(within, cnt, float(CAP), None, ALU.is_lt))
            link(nc.gpsimd.tensor_tensor(flat(g.CW[:, :, :]), flat(g.CW[:, :, :]), within, ALU.mult))
            link(nc.gpsimd.tensor_scalar(start, flat(g.idx[:, :, :]), float(E), float(CAP), ALU.add, ALU.mult))
            link(nc.gpsimd.tensor_tensor(w1, start, cnt, ALU.add))
            link(nc.gpsimd.tensor_tensor(w1, w1, g.iof[:, E:], ALU.subtract))
            link(nc.gpsimd.tensor_tensor(w1, w1, within, ALU.mult))
            link(nc.gpsimd.tensor_tensor(w1, w1, g.iof[:, E:], ALU.add))
            link(nc.gpsimd.tensor_copy(g.rows_out[:, :], w1))
            link(nc.gpsimd.tensor_scalar(w2, cnt, float(CAP - 1), None, ALU.min))
            link(nc.gpsimd.tensor_tensor(w2, w2, start, ALU.add))
            link(nc.gpsimd.tensor_copy(g.ROW[:, :], w2))
            for k in range(TOPK):
                for t in range(NT):
                    n = k * NT + t
                    pool.indirect_dma_start(g.x_disp[:, :], bass.IndirectOffsetOnAxis(g.rows_out[:, n:n + 1], 0),
                                            g.XN[:, t, :], None).then_inc(sem("dispatched"), 16)
            pool.wait_ge(sem("dispatched"), 16 * TOPK * NT)

        @block.vector
        def _(dve):
            nc.vector.memset(twin[:, :], 0.0).then_inc(sem("i_twin"), 1)
            dve.wait_ge(sem("i_twin"), 1)
            for half in halves:
                nc.vector.memset(twin[half, half], 1.0).then_inc(sem("i_twin"), 1)
            for half in halves:
                nc.vector.tensor_copy(eye2[half, :], g.ident[half, half]).then_inc(sem("i_eyes"), 1)
            for i, f in enumerate((7.0, 15.0, 13.0)):
                nc.vector.tensor_scalar(eyes[:, i, :], g.ident[:, :], f, None, ALU.mult).then_inc(sem("i_eyes"), 1)
            dve.wait_ge(sem("i_eyes"), 5)
            link = Link(dve, sem("dve_step"), start=g.dve_steps)
            dve.wait_ge(sem("i_colsum"), 1)
            link(nc.vector.reduce_max(den[:, :], g.bank(0, 4).rearrange("p (n c) -> p n c", c=LM), AX.X))
            nc.vector.reciprocal(den[:, :], den[:, :]).then_inc(sem("i_den"), 1)
            dve.wait_ge(sem("i_den"), 1)
            nc.vector.tensor_tensor(AQ[:, :, LM:P], eye2[:, :].unsqueeze(1).broadcast_to([P, NPAIR, LM]),
                                    over_last(den[:, :], LM), ALU.mult).then_inc(sem("i_den"), 1)
            for n in range(NG):
                dve.wait_ge(sem("i_gram"), n + 1)
                nc.vector.tensor_tensor(grp(A, n), bankg(n), over_last(den[:, n * GR:(n + 1) * GR], P), ALU.mult)\
                  .then_inc(sem("i_dve"), 2)
                dve.wait_ge(sem("i_dve"), 3 * n + 2)
                nc.vector.scalar_tensor_tensor(grp(X, n), grp(A, n), -1.0, eye(0), ALU.mult, ALU.add)\
                  .then_inc(sem("i_dve"), 1)
            g.dve_steps = link.n
            with dve.Fori(0, ITERS) as it:
                for stage in range(2):
                    for n in range(NG):
                        dve.wait_ge(sem("i_mm"), at(it, MM0, stage * NG + n + 1))
                        nc.vector.scalar_tensor_tensor(grp(X, n), bankg(n), -1.0, eye(1 + stage), ALU.mult, ALU.add)\
                          .then_inc(sem("i_dve"), 1)
                for n in range(NG):
                    dve.wait_ge(sem("i_act"), at(it, AC, AC + 2 * n + 1))
                    for half in halves:
                        last = nc.vector.scalar_tensor_tensor(grp(X, n)[half, :, half], grp(AQ, n)[half, :, 0:LM], -1.0,
                                                              eye(0)[half, :, half], ALU.mult, ALU.add)
                    last.then_inc(sem("i_dve"), 1)

        @block.scalar
        def _(act):
            act.wait_ge(sem("r_counts"), 2)
            for i, k in ((0, 6), (1, 6), (3, 7)):
                act.activation(tot[:, i, :, :], g.bank(k).rearrange("p (n e) -> p n e", e=E), ACT.Copy)\
                   .then_inc(sem("r_counted"), 1)
            for n in range(NG):
                act.wait_ge(sem("i_kt_ps"), n + 1)
                act.activation(grp(X, n), g.bank(4 + n % 2).rearrange("p (n c) -> p n c", c=P), ACT.Copy)\
                   .then_inc(sem("i_act"), 1)
            for n in range(NG):
                act.wait_ge(sem("i_dve"), 3 * n + 2)
                for half in halves:
                    last = act.activation(grp(AQ, n)[half, :, 0:LM], grp(A, n)[half, :, half], ACT.Copy)
                last.then_inc(sem("i_act"), 1)
            with act.Fori(0, ITERS) as it:
                for n in range(NG):
                    act.wait_ge(sem("i_mm"), at(it, MM0, 2 * NG + n + 1))
                    act.activation(grp(AQ, n), bankg(n), ACT.Copy, scale=0.25).then_inc(sem("i_act"), 1)
                    for half in halves:
                        last = act.activation(grp(A, n)[half, :, half], bankg(n)[half, :, 0:LM], ACT.Copy, scale=0.25)
                    last.then_inc(sem("i_act"), 1)
            act.wait_ge(sem("i_act"), AC * (ITERS + 1))
            for n in range(NG):
                for half in halves:
                    last = act.activation(grp(A, n)[half, :, half], grp(AQ, n)[half, :, LM:P], ACT.Copy)
                last.then_inc(sem("i_q"), 1)
            act.wait_ge(sem("i_z"), 1)
            act.activation(z[:, 0:NPAIR, :], firsts, ACT.Copy).then_inc(sem("i_z_out"), 1)
            act.wait_ge(sem("i_w"), 1)
            act.wait_ge(sem("i_wm"), 2)
            w = firsts.rearrange("p (j r) d -> p j r d", r=2)
            wm = g.WM[:, :, :].rearrange("p (j r) c -> p j r c", r=2)
            for r in range(2):
                for i, half in enumerate(halves):
                    c = 16 * r + HD * i
                    act.activation(wm[half, :, r, c:c + HD], w[half, :, r, :], ACT.Copy).then_inc(sem("i_wm"), 1)

        @block.tensor
        def _(pe):
            def products(n, lhs, rhs, name="i_mm"):
                for i in range(GR):
                    p = n * GR + i
                    last = nc.tensor.matmul(bankg(n)[:, i, :], lhs[:, p, :], rhs[:, p, :], start=True, stop=True)
                last.then_inc(sem(name), 1)

            both = g.oh[:, :, :, :].rearrange("p k n e -> p (k n e)")
            nc.tensor.matmul(g.bank(7), g.upper[:, :], both, start=True, stop=True).then_inc(sem("r_counts"), 1)
            nc.tensor.matmul(g.bank(6), g.ones[:, :], both, start=True, stop=True).then_inc(sem("r_counts"), 1)
            pe.wait_ge(sem("i_twin"), 3)
            for j in range(4):
                last = nc.tensor.matmul(g.bank(j), twin[:, :], g.KS[:, 8 * j:8 * j + 8, :].rearrange("p n c -> p (n c)"),
                                        start=True, stop=True)
            last.then_inc(sem("i_colsum"), 1)
            for n in range(NG):
                if n >= 2:
                    pe.wait_ge(sem("i_act"), n - 1)
                for i in range(GR):
                    last = nc.tensor.transpose(g.ps[:, (4 + n % 2) * BANK + i * P:(4 + n % 2) * BANK + i * P + P],
                                               kb[:, n * GR + i, :], g.ident[:, :])
                last.then_inc(sem("i_kt_ps"), 1)
            pe.wait_ge(sem("i_den"), 1)
            pe.wait_ge(sem("i_act"), NG)
            pe.wait_ge(sem("r_counted"), 3)
            for n in range(NG):
                products(n, X, X, "i_gram")
            pe.wait_ge(sem("i_den"), 2)
            with pe.Fori(0, ITERS) as it:
                for n in range(NG):
                    pe.wait_ge(sem("i_act"), at(it, AC, 2 * n + 2))
                    pe.wait_ge(sem("i_dve"), at(it, DV, 2 * NG + n + 1))
                    products(n, A, X)
                for n in range(NG):
                    pe.wait_ge(sem("i_dve"), at(it, DV, DV + n + 1))
                    products(n, A, X)
                pe.wait_ge(sem("i_act"), at(it, AC, AC))
                for n in range(NG):
                    pe.wait_ge(sem("i_dve"), at(it, DV, DV + NG + n + 1))
                    products(n, X, AQ)
            for n in range(NG):
                pe.wait_ge(sem("i_q"), n + 1)
                for p in range(n * GR, n * GR + GR):
                    last = nc.tensor.matmul(g.ps[:, p * P:(p + 1) * P], A[:, p, :],
                                            g.NV[:, p:p + WIDE, :].rearrange("p n d -> p (n d)"), start=True, stop=True)
            last.then_inc(sem("i_z"), 1)
            pe.wait_ge(sem("i_z_out"), 1)
            pe.wait_ge(sem("i_wm"), 2)
            for p in range(NPAIR):
                last = nc.tensor.matmul(g.ps[:, p * P:(p + 1) * P], kb[:, p, :],
                                        z[:, p:p + WIDE, :].rearrange("p n d -> p (n d)"), start=True, stop=True)
            last.then_inc(sem("i_w"), 1)


def layer1_attention(g):
    nc, sem = g.nc, g.sem
    QS = 4
    with ExitStack() as mem:
        sb = lambda name, shape, dt=F32: mem.enter_context(nc.sbuf_tensor(name, shape, dt))
        qs = sb("f_q", [P, QS, P])
        klm = sb("f_klm", [P, B, H, LM])
        wm = sb("f_wm", [P, QS, PAIRS, 32])
        sums = sb("f_sums", [P, 2, 32])
        mh = sb("f_max", [P, 2, H])
        lx = sb("f_lx", [P, 2, H, LM])
        le = sb("f_le", [P, 2, H, LM])
        lT = sb("f_lT", [P, 2, PAIRS, P])
        rec = sb("f_rec", [P, P])
        yT = sb("f_yT", [P, 2, P])
    NUM, DEN, OUT = g.bank(6)[:, 0:P], g.bank(6)[:, P:2 * P], g.bank(7)[:, 0:P]
    cnt = lambda b, t: at(b, TB, t + 1)
    AFTER_T, AFTER_Y, AFTER_P = 2, 3, 4

    def turns(eng, step, behind):
        for t in range(TB):
            step(0, t, True, t)
        with eng.Fori(1, B) as b:
            for t in range(TB):
                step(b, t, True, TB)
        for t in range(behind):
            step(B, t, False, TB)

    with nc.Block() as block:

        @block.sync
        def _(sp):
            def load(b, t):
                if not (isinstance(b, int) and b == 0 and t < QS):
                    sp.wait_ge(sem("f_scores"), cnt(b, t - QS))
                sp.dma_start(qs[:, t % QS, :], g.q1_keep[bass.ds(b, 1), :, t * P:(t + 1) * P]
                             .rearrange("a p t -> (a p) t")).then_inc(sem(f"f_q{t % QS}"), 16)

            turns(sp, lambda b, t, own, before: load(b, t), 0)

        @block.vector
        def _(dve):
            nc.vector.memset(sums[:, :, :], 0.0).then_inc(sem("f_sums"), 1)
            dve.wait_ge(sem("f_sums"), 1)
            for r in range(2):
                for i in range(2):
                    c = 16 * r + HD * i
                    nc.vector.memset(sums[LM * i:LM * i + LM, r, c:c + HD], 1.0).then_inc(sem("f_sums"), 1)
            for b in range(B):
                nc.vector.tensor_tensor(klm[:, b, :, :], *heads_of(g.KL[:, b, :], g.headmask[:, :], LM), ALU.mult)\
                  .then_inc(sem("f_klm"), 1)

            def step(b, t, own, before):
                if own:
                    s = t % 2
                    ps = g.bank(2 * s, 2).rearrange("p (h n) -> p h n", n=LM)
                    dve.wait_ge(sem("f_scores"), cnt(b, t))
                    nc.vector.reduce_max(mh[:, s, :], ps, AX.X).then_inc(sem("f_max"), 1)
                    dve.wait_ge(sem("f_max"), cnt(b, t))
                    if before >= 2:
                        dve.wait_ge(sem("f_le"), cnt(b, t - 2))
                    nc.vector.tensor_tensor(lx[:, s, :, :], ps, over_last(mh[:, s, :], LM), ALU.subtract)\
                      .then_inc(sem("f_lx"), 1)
                if before >= AFTER_Y:
                    n = t - AFTER_Y
                    dve.wait_ge(sem("f_y"), cnt(b, n))
                    nc.vector.reciprocal(rec[:, :], DEN).then_inc(sem("f_rec"), 1)
                    dve.wait_ge(sem("f_rec"), cnt(b, n))
                    if before >= AFTER_Y + 2:
                        dve.wait_ge(sem("f_s"), cnt(b, n - 2))
                    nc.vector.tensor_tensor(yT[:, n % 2, :], NUM, rec[:, :], ALU.mult).then_inc(sem("f_yT"), 1)

            turns(dve, step, AFTER_Y)

        @block.scalar
        def _(act):
            def step(b, t, own, before):
                if own:
                    s = t % 2
                    act.wait_ge(sem("f_lx"), cnt(b, t))
                    if before >= 2:
                        act.wait_ge(sem("f_lT_ps"), cnt(b, t - 2))
                    act.activation(le[:, s, :, :], lx[:, s, :, :], ACT.Exp).then_inc(sem("f_le"), 1)
                if before >= AFTER_T:
                    n = t - AFTER_T
                    act.wait_ge(sem("f_lT_ps"), cnt(b, n))
                    if before >= AFTER_T + 2:
                        act.wait_ge(sem("f_y"), cnt(b, n - 2))
                    act.activation(lT[:, n % 2, :, :], g.bank(4, 2).rearrange("p (n c) -> p n c", c=P), ACT.Copy)\
                       .then_inc(sem("f_lT"), 1)
                if before >= AFTER_P:
                    n = t - AFTER_P
                    act.wait_ge(sem("f_s"), cnt(b, n))
                    act.activation(g.G[:, bass.ds(b * TB + n, 1), :].rearrange("p a d -> p (a d)"), OUT, ACT.Copy)\
                       .then_inc(sem("f_out"), 1)
                if own:
                    act.activation(wm[:, t % QS, :, :], g.WM[:, bass.ds(b * PAIRS, PAIRS), :], ACT.Copy)\
                       .then_inc(sem("f_wm"), 1)

            for t in range(TB):
                step(0, t, True, t)
            with act.Fori(1, B) as b:
                for t in range(TB):
                    step(b, t, True, TB)
            for t in range(AFTER_P):
                if t < AFTER_T:
                    step(B, t, False, TB)
                else:
                    n = t - AFTER_P
                    act.wait_ge(sem("f_s"), cnt(B, n))
                    act.activation(g.G[:, B * TB + n, :], OUT, ACT.Copy).then_inc(sem("f_out"), 1)

        @block.tensor
        def _(pe):
            pe.wait_ge(sem("f_klm"), B)
            pe.wait_ge(sem("f_sums"), 5)

            def step(b, t, own, before):
                if own:
                    pe.wait_ge(sem(f"f_q{t % QS}"), at(b, 16 * TB // QS, 16 * (t // QS + 1)))
                    if before >= 2:
                        pe.wait_ge(sem("f_lx"), cnt(b, t - 2))
                    for j in range(2):
                        rhs = klm[:, bass.ds(b, 1), 8 * j:8 * j + 8, :].rearrange("p a h n -> p (a h n)")
                        last = nc.tensor.matmul(g.bank(2 * (t % 2) + j), qs[:, t % QS, :], rhs, start=True, stop=True)
                    last.then_inc(sem("f_scores"), 1)
                if before >= AFTER_T and (own or t < AFTER_T):
                    n = t - AFTER_T
                    pe.wait_ge(sem("f_le"), cnt(b, n))
                    if before >= AFTER_T + 1:
                        pe.wait_ge(sem("f_lT"), cnt(b, n - 1))
                    for p in range(PAIRS):
                        last = nc.tensor.transpose(g.ps[:, 4 * BANK + p * P:4 * BANK + (p + 1) * P],
                                                   le[:, n % 2, 2 * p:2 * p + 2, :].rearrange("p h n -> p (h n)"),
                                                   g.ident[:, :])
                    last.then_inc(sem("f_lT_ps"), 1)
                if before >= AFTER_Y and (own or t < AFTER_Y):
                    n = t - AFTER_Y
                    pe.wait_ge(sem("f_lT"), cnt(b, n))
                    pe.wait_ge(sem("f_wm"), cnt(b, n))
                    if before >= AFTER_Y + 1:
                        pe.wait_ge(sem("f_yT"), cnt(b, n - 1))
                    for dst, by in ((NUM, lambda p: wm[:, n % QS, p, :]), (DEN, lambda p: sums[:, p % 2, :])):
                        for r in range(2):
                            for j in range(4):
                                last = nc.tensor.matmul(dst[32 * j:32 * j + 32, :], by(2 * j + r),
                                                        lT[:, n % 2, 2 * j + r, :], start=(r == 0), stop=(r == 1))
                    last.then_inc(sem("f_y"), 1)
                if before >= AFTER_P:
                    n = t - AFTER_P
                    pe.wait_ge(sem("f_yT"), cnt(b, n))
                    if before >= AFTER_P + 1:
                        pe.wait_ge(sem("f_out"), cnt(b, n - 1))
                    nc.tensor.matmul(OUT, yT[:, n % 2, :], g.wproj1[:, :], start=True, stop=True)\
                      .then_inc(sem("f_s"), 1)

            turns(pe, step, AFTER_P)


XT = -(-CAP // P)
LASTROWS = CAP - (XT - 1) * P
CHUNKS = [(i * CAP // 3, (i + 1) * CAP // 3) for i in range(3)]


def experts(g):
    nc, sem = g.nc, g.sem
    with ExitStack() as mem:
        sb = lambda name, shape, dt=F32: mem.enter_context(nc.sbuf_tensor(name, shape, dt))
        xe = [sb(f"e_x{c}", [P, XT, D]) for c in range(2)]
        w1 = [sb(f"e_w1{c}", [P, HID]) for c in range(2)]
        w2 = [sb(f"e_w2{c}", [P, HC, D]) for c in range(2)]
        b1 = [sb(f"e_b1{c}", [P, HC]) for c in range(2)]
        b2 = [sb(f"e_b2{c}", [P, D]) for c in range(2)]
        xT = sb("e_xT", [P, CAP])
        hT = [sb(f"e_hT{c}", [P, HC, CAP]) for c in range(2)]
        y = [sb(f"e_y{c}", [P, XT, D]) for c in range(2)]
        credit = sb("e_credit", [P, 2])
    NCH = len(CHUNKS)
    LOADS = 16 * 5
    ex = lambda j, per, c, n: j * (2 * per) + (c * per + n)
    rows = lambda t: P if t < XT - 1 else LASTROWS

    with nc.Block() as block:

        @block.sync
        def _(sp):
            def load(j, c):
                one = bass.ds(j * 2 + c, 1)
                flat = lambda ap: ap.rearrange("a p n -> (a p) n")
                first = (j * 2 + c) * CAP
                s = f"e_loaded{c}"
                sp.dma_start(xe[c][:, 0:XT - 1, :],
                             g.x_disp[bass.ds(first, (XT - 1) * P), :].rearrange("(t p) d -> p t d", p=P))\
                  .then_inc(sem(s), 16)
                sp.dma_start(xe[c][0:LASTROWS, XT - 1, :], g.x_disp[bass.ds(first + (XT - 1) * P, LASTROWS), :])\
                  .then_inc(sem(s), 16)
                sp.dma_start(w1[c][:, :], flat(g.W1[one, :, :])).then_inc(sem(s), 16)
                sp.dma_start(w2[c][:, :, :], g.W2[one, :, :].rearrange("a (c p) d -> (a p) c d", p=P))\
                  .then_inc(sem(s), 16)
                sp.dma_start(b2[c][:, :], g.b2[one, :].broadcast_to([P, D])).then_inc(sem(s), 16)

            def store(j, c):
                sp.wait_ge(sem("e_y"), ex(j, 3, c, 3))
                first = (j * 2 + c) * CAP
                sp.dma_start(g.y_exp[bass.ds(first, (XT - 1) * P), :].rearrange("(t p) d -> p t d", p=P),
                             y[c][:, 0:XT - 1, :]).then_inc(sem(f"e_stored{c}"), 16)
                sp.dma_start(g.y_exp[bass.ds(first + (XT - 1) * P, LASTROWS), :], y[c][0:LASTROWS, XT - 1, :])\
                  .then_inc(sem(f"e_stored{c}"), 16)

            for c in range(2):
                load(0, c)
            with sp.Fori(0, E // 2 - 1) as j:
                for c in range(2):
                    store(j, c)
                    load(j + 1, c)
            for c in range(2):
                store(E // 2 - 1, c)
                sp.wait_ge(sem(f"e_stored{c}"), 32 * (E // 2 + 1))

        @block.gpsimd
        def _(pool):
            for c in range(2):
                nc.gpsimd.memset(credit[:, c:c + 1], 0.0).then_inc(sem(f"e_stored{c}"), 32)

        @block.vector
        def _(dve):
            with dve.Fori(0, E // 2) as j:
                for c in range(2):
                    nc.vector.tensor_copy(b1[c][:, :], g.b1T[:, bass.ds((j * 2 + c) * HC, HC)]).then_inc(sem("e_b1"), 1)
                    for i in range(3):
                        n = 4 if i < 2 else 1
                        r = P if i < 2 else LASTROWS
                        w = n * P if i < 2 else LASTROWS
                        dve.wait_ge(sem("e_xT_ps"), ex(j, 3, c, i + 1))
                        nc.vector.tensor_copy(xT[:, i * BANK:i * BANK + w], g.ps[:, i * BANK:i * BANK + w])\
                          .then_inc(sem("e_xT"), 1)
                    dve.wait_ge(sem(f"e_stored{c}"), j * 32 + 32)
                    for i in range(3):
                        n = 4 if i < 2 else 1
                        r = P if i < 2 else LASTROWS
                        dve.wait_ge(sem("e_y_ps"), ex(j, 3, c, i + 1))
                        nc.vector.tensor_tensor(y[c][0:r, 4 * i:4 * i + n, :],
                                                g.ps[0:r, (6 + i % 2) * BANK:(6 + i % 2) * BANK + n * P]
                                                .rearrange("p (n c) -> p n c", c=P),
                                                b2[c][0:r, :].unsqueeze(1).broadcast_to([r, n, D]), ALU.add)\
                          .then_inc(sem("e_y"), 1)

        @block.scalar
        def _(act):
            with act.Fori(0, E // 2) as j:
                for c in range(2):
                    act.wait_ge(sem("e_b1"), ex(j, 1, c, 1))
                    for i in range(HC):
                        for m, (lo, hi) in enumerate(CHUNKS):
                            n = i * NCH + m
                            act.wait_ge(sem("e_h_ps"), ex(j, HC * NCH, c, n + 1))
                            act.activation(hT[c][:, i, lo:hi], g.ps[:, (3 + n % 3) * BANK:(3 + n % 3) * BANK + hi - lo],
                                           ACT.Gelu, bias=b1[c][:, i:i + 1]).then_inc(sem("e_h"), 1)

        @block.tensor
        def _(pe):
            with pe.Fori(0, E // 2) as j:
                for c in range(2):
                    pe.wait_ge(sem(f"e_loaded{c}"), j * LOADS + LOADS)
                    for t in range(XT):
                        last = nc.tensor.transpose(g.ps[:, t * P:t * P + rows(t)], xe[c][0:rows(t), t, :],
                                                   g.ident[0:rows(t), 0:rows(t)])
                        if t % 4 == 3 or t == XT - 1:
                            last.then_inc(sem("e_xT_ps"), 1)
                    pe.wait_ge(sem("e_xT"), ex(j, 3, c, 3))
                    for i in range(HC):
                        for m, (lo, hi) in enumerate(CHUNKS):
                            n = i * NCH + m
                            if n >= 3:
                                pe.wait_ge(sem("e_h"), ex(j, HC * NCH, c, n - 2))
                            nc.tensor.matmul(g.ps[:, (3 + n % 3) * BANK:(3 + n % 3) * BANK + hi - lo],
                                             w1[c][:, i * P:(i + 1) * P], xT[:, lo:hi], start=True, stop=True)\
                              .then_inc(sem("e_h_ps"), 1)
                    pe.wait_ge(sem("e_h"), ex(j, HC * NCH, c, HC * NCH))
                    for t in range(XT):
                        r = rows(t)
                        if t == 2 * 4:
                            pe.wait_ge(sem("e_y"), ex(j, 3, c, 1))
                        col = (6 + t // 4 % 2) * BANK + t % 4 * P
                        for i in range(HC):
                            last = nc.tensor.matmul(g.ps[0:r, col:col + D], hT[c][:, i, t * P:t * P + r], w2[c][:, i, :],
                                                    start=(i == 0), stop=(i == HC - 1))
                        if t % 4 == 3 or t == XT - 1:
                            last.then_inc(sem("e_y_ps"), 1)
                    pe.wait_ge(sem("e_y"), ex(j, 3, c, 3))


def combine(g):
    nc, sem = g.nc, g.sem
    with ExitStack() as mem:
        sb = lambda name, shape, dt=F32: mem.enter_context(nc.sbuf_tensor(name, shape, dt))
        yk = sb("g_y", [P, TOPK, NT, D])
        f = sb("g_f", [P, NT, D])
        sg = sb("g_sg", [P, NT, D])
    with nc.Block() as block:

        @block.gpsimd
        def _(pool):
            for t in range(NT):
                for k in range(TOPK):
                    n = k * NT + t
                    pool.indirect_dma_start(yk[:, k, t, :], None, g.y_exp[:, :],
                                            bass.IndirectOffsetOnAxis(g.ROW[:, n:n + 1], 0))\
                        .then_inc(sem(f"g_gathered{t // TB}"), 16)

        @block.vector
        def _(dve):
            link = Link(dve, sem("dve_step"), start=g.dve_steps)

            def finish(b):
                s = slice(b * TB, (b + 1) * TB)
                dve.wait_ge(sem("g_sg"), b + 1)
                link(nc.vector.tensor_tensor(f[:, s, :], f[:, s, :], sg[:, s, :], ALU.mult))
                link(nc.vector.tensor_tensor(f[:, s, :], f[:, s, :], g.G[:, s, :], ALU.mult))
                nc.vector.tensor_tensor(g.X[:, s, :], g.X[:, s, :], f[:, s, :], ALU.add).then_inc(sem("g_x"), 1)

            for b in range(B):
                s = slice(b * TB, (b + 1) * TB)
                dve.wait_ge(sem(f"g_gathered{b}"), 16 * TOPK * TB)
                for k in range(TOPK):
                    link(nc.vector.tensor_tensor(yk[:, k, s, :], yk[:, k, s, :], over_last(g.CW[:, k, s], D), ALU.mult))
                nc.vector.tensor_tensor(f[:, s, :], yk[:, 0, s, :], yk[:, 1, s, :], ALU.add).then_inc(sem("g_f"), 1)
                dve.wait_ge(sem("g_f"), b + 1)
                if b >= 1:
                    finish(b - 1)
            finish(B - 1)

        @block.scalar
        def _(act):
            for b in range(B):
                s = slice(b * TB, (b + 1) * TB)
                act.wait_ge(sem("g_f"), b + 1)
                act.activation(sg[:, s, :], f[:, s, :], ACT.Sigmoid).then_inc(sem("g_sg"), 1)

        @block.sync
        def _(sp):
            dst = g.out.rearrange("b (n p) d -> p (b n) d", p=P)
            for b in range(B):
                s = slice(b * TB, (b + 1) * TB)
                sp.wait_ge(sem("g_x"), b + 1)
                sp.dma_start(dst[:, s, :], g.X[:, s, :]).then_inc(sem("out_stored"), 16)
            sp.wait_ge(sem("out_stored"), 16 * B)


def two_layers(nc, *ins):
    with ExitStack() as ctx:
        g = make(nc, ctx, ins)
        setup(g, ctx)
        layer0_inputs(g)
        layer0_attention(g)
        layer0_outputs(g)
        inverse_and_routing(g)
        layer1_attention(g)
        experts(g)
        combine(g)


_INS = ['L0_attn_z', 'L0_attn_ln_scale', 'L0_attn_ln_bias', 'L0_attn_w_qkv', 'L0_attn_w_proj', 'L0_attn_b_proj',
        'L0_ffn_W_r', 'L0_ffn_W_k', 'L0_ffn_W_v', 'L0_ffn_mu_r', 'L0_ffn_mu_k', 'L1_attn_W_attn', 'L1_attn_W_proj',
        'L1_ffn_Wg', 'L1_ffn_W1', 'L1_ffn_b1', 'L1_ffn_W2', 'L1_ffn_b2']
_OUTS = [((B, T, D), 'float32')]


def kernel(**inputs):
    import numpy as _np
    import concourse.bacc as _bacc
    from concourse import mybir as _mybir
    from concourse.bass_utils import run_bass_kernel_spmd as _run

    nc = _bacc.Bacc("TRN2", target_bir_lowering=False, num_devices=1)
    arrays, args = {}, []
    for name in _INS:
        a = _np.ascontiguousarray(inputs[name])
        arrays[f"in_{name}_dram"] = a
        args.append(nc.dram_tensor(f"in_{name}_dram", a.shape, _mybir.dt.from_np(a.dtype), kind="ExternalInput").ap())
    for i, (shape, dtype) in enumerate(_OUTS):
        dt = _mybir.dt.from_np(_np.dtype(dtype))
        args.append(nc.dram_tensor(f"out_{i}_dram", shape, dt, kind="ExternalOutput").ap())
    two_layers(nc, *args)
    r = _run(nc, [arrays], core_ids=[0])
    got = tuple(r.results[0][f"out_{i}_dram"] for i in range(len(_OUTS)))
    return got[0]
```
